# Optimizing a Trainium2 kernel written in Bass

```python
import numpy as np
import jax
import jax.numpy as jnp

def _softmax(x, axis=-1):
    return jax.nn.softmax(x, axis=axis)

def _gelu(x):
    return jax.nn.gelu(x, approximate=True)

def _silu(x):
    return jax.nn.silu(x)

def _sigmoid(x):
    return jax.nn.sigmoid(x)

def _layernorm(x, axis=-1, eps=1e-05):
    m = jnp.mean(x, axis=axis, keepdims=True)
    v = jnp.var(x, axis=axis, keepdims=True)
    return (x - m) / jnp.sqrt(v + eps)

def _scatter_add(tgt, idx, src, axis=0):
    return tgt.at[idx].add(src)

def _segment_sum(src, seg, n):
    return jax.ops.segment_sum(src, seg, n)
kernel_name = 'mk_seq_preln_d1_jaxref_r8_adc419'

def setup_inputs(seed: int=0):
    np.random.seed(seed)
    _w = jnp.asarray

    def _L0_attn_setup():
        import jax, jax.numpy as jnp
        import numpy as np
        key = jax.random.key(seed)
        B, L, d_model, d_state, expand = (2, 256, 128, 16, 2)
        d_inner = expand * d_model
        ks = jax.random.split(key, 8)
        s = lambda k, shape, scale: jax.random.normal(k, shape, dtype=jnp.float32) * scale
        x = s(ks[0], (B, L, d_model), 1.0)
        W_in = s(ks[1], (d_model, 2 * d_inner), 0.02)
        W_delta = s(ks[2], (d_inner, d_inner), 0.02)
        b_delta = s(ks[3], (d_inner,), 0.02)
        W_B = s(ks[4], (d_inner, d_state), 0.02)
        W_C = s(ks[5], (d_inner, d_state), 0.02)
        A_log = jnp.log(jnp.broadcast_to(jnp.arange(1, d_state + 1, dtype=jnp.float32), (d_inner, d_state)))
        D_param = jnp.ones((d_inner,), dtype=jnp.float32)
        W_out = s(ks[6], (d_inner, d_model), 0.02)
        return dict(x=x, W_in=W_in, W_delta=W_delta, b_delta=b_delta, W_B=W_B, W_C=W_C, A_log=A_log, D_param=D_param, W_out=W_out)
    _L0_attn_in = _L0_attn_setup()

    def _L0_ffn_setup():
        import jax, jax.numpy as jnp
        import numpy as np
        E, K = (8, 4)
        B, S, D = (4, 128, 128)
        H = D * 2 * 4 // 3

        def _swiglu(u, w1, w2, w3):
            h = jnp.einsum('...d,hd->...h', u, w1)
            v = jnp.einsum('...d,hd->...h', u, w2)
            return jnp.einsum('...h,dh->...d', jax.nn.sigmoid(h) * h * v, w3)
        key = jax.random.key(seed)
        ks = jax.random.split(key, 9)
        std = 0.02
        return {'x': jax.random.normal(ks[0], (B, S, D), jnp.float32), 'Wg': jax.random.normal(ks[1], (E, D), jnp.float32) * std, 'routing_bias': jnp.zeros((E,), jnp.float32), 'W1': jax.random.normal(ks[2], (E, H, D), jnp.float32) * std, 'W2': jax.random.normal(ks[3], (E, H, D), jnp.float32) * std, 'W3': jax.random.normal(ks[4], (E, D, H), jnp.float32) * std, 'Ws1': jax.random.normal(ks[5], (H, D), jnp.float32) * std, 'Ws2': jax.random.normal(ks[6], (H, D), jnp.float32) * std, 'Ws3': jax.random.normal(ks[7], (D, H), jnp.float32) * std}
    _L0_ffn_in = _L0_ffn_setup()
    _d = {'L0_attn_x': _L0_attn_in['x'], 'L0_attn_W_in': _L0_attn_in['W_in'], 'L0_attn_W_delta': _L0_attn_in['W_delta'], 'L0_attn_b_delta': _L0_attn_in['b_delta'], 'L0_attn_W_B': _L0_attn_in['W_B'], 'L0_attn_W_C': _L0_attn_in['W_C'], 'L0_attn_A_log': _L0_attn_in['A_log'], 'L0_attn_D_param': _L0_attn_in['D_param'], 'L0_attn_W_out': _L0_attn_in['W_out'], 'L0_ffn_Wg': _L0_ffn_in['Wg'], 'L0_ffn_routing_bias': _L0_ffn_in['routing_bias'], 'L0_ffn_W1': _L0_ffn_in['W1'], 'L0_ffn_W2': _L0_ffn_in['W2'], 'L0_ffn_W3': _L0_ffn_in['W3'], 'L0_ffn_Ws1': _L0_ffn_in['Ws1'], 'L0_ffn_Ws2': _L0_ffn_in['Ws2'], 'L0_ffn_Ws3': _L0_ffn_in['Ws3']}
    _x0 = _d['L0_attn_x']
    _d['L0_attn_x'] = jax.random.normal(jax.random.fold_in(jax.random.key(seed), 1), (32, 256, 128), dtype=_x0.dtype)
    del _x0
    return _d

def reference(L0_attn_x, L0_attn_W_in, L0_attn_W_delta, L0_attn_b_delta, L0_attn_W_B, L0_attn_W_C, L0_attn_A_log, L0_attn_D_param, L0_attn_W_out, L0_ffn_Wg, L0_ffn_routing_bias, L0_ffn_W1, L0_ffn_W2, L0_ffn_W3, L0_ffn_Ws1, L0_ffn_Ws2, L0_ffn_Ws3):

    def _L0_attn_ref(x, W_in, W_delta, b_delta, W_B, W_C, A_log, D_param, W_out):
        import jax, jax.numpy as jnp
        import numpy as np
        d_inner = W_delta.shape[0]
        x_and_res = x @ W_in
        u, res = (x_and_res[..., :d_inner], x_and_res[..., d_inner:])
        u = jax.nn.silu(u)
        delta = jax.nn.softplus(u @ W_delta + b_delta)
        Bm = u @ W_B
        Cm = u @ W_C
        A = -jnp.exp(A_log)

        def step(h, inp):
            d_t, B_t, C_t, u_t = inp
            dA = jnp.exp(d_t[..., None] * A)
            h = dA * h + d_t[..., None] * B_t[:, None, :] * u_t[..., None]
            y_t = jnp.einsum('bdn,bn->bd', h, C_t)
            return (h, y_t)
        Bsz = x.shape[0]
        h0 = jnp.zeros((Bsz, d_inner, A.shape[1]), dtype=x.dtype)
        xs = (jnp.swapaxes(delta, 0, 1), jnp.swapaxes(Bm, 0, 1), jnp.swapaxes(Cm, 0, 1), jnp.swapaxes(u, 0, 1))
        _, ys = jax.lax.scan(step, h0, xs)
        y = jnp.swapaxes(ys, 0, 1) + u * D_param
        y = y * jax.nn.silu(res)
        return y @ W_out

    def _L0_ffn_ref(x, Wg, routing_bias, W1, W2, W3, Ws1, Ws2, Ws3):
        import jax, jax.numpy as jnp
        import numpy as np
        E, K = (8, 4)
        B, S, D = (4, 128, 128)
        H = D * 2 * 4 // 3

        def _swiglu(u, w1, w2, w3):
            h = jnp.einsum('...d,hd->...h', u, w1)
            v = jnp.einsum('...d,hd->...h', u, w2)
            return jnp.einsum('...h,dh->...d', jax.nn.sigmoid(h) * h * v, w3)
        gate = jnp.einsum('bsd,ed->bse', x, Wg) + routing_bias
        _, top_idx = jax.lax.top_k(gate, K)
        mask = jax.nn.one_hot(top_idx, E, dtype=gate.dtype).sum(-2)
        masked_gate = jnp.where(mask > 0, gate, -jnp.inf)
        probs = jax.nn.softmax(masked_gate, axis=-1)
        weights = probs * mask
        out = _swiglu(x, Ws1, Ws2, Ws3)
        h1 = jnp.einsum('bsd,ehd->ebsh', x, W1)
        h2 = jnp.einsum('bsd,ehd->ebsh', x, W2)
        eo = jnp.einsum('ebsh,edh->ebsd', jax.nn.sigmoid(h1) * h1 * h2, W3)
        out = out + jnp.einsum('ebsd,bse->bsd', eo, weights)
        return out
    x = L0_attn_x
    x = x + _L0_attn_ref(_layernorm(x, axis=-1), L0_attn_W_in, L0_attn_W_delta, L0_attn_b_delta, L0_attn_W_B, L0_attn_W_C, L0_attn_A_log, L0_attn_D_param, L0_attn_W_out)
    x = x + _L0_ffn_ref(_layernorm(x, axis=-1), L0_ffn_Wg, L0_ffn_routing_bias, L0_ffn_W1, L0_ffn_W2, L0_ffn_W3, L0_ffn_Ws1, L0_ffn_Ws2, L0_ffn_Ws3)
    return x

_drawn_inputs = setup_inputs


def setup_inputs(seed=0):
    import zlib

    import numpy as np

    out = dict(_drawn_inputs(seed))
    spreads = {'L0_attn_D_param': (1.0, 0.6), 'L0_ffn_routing_bias': (0.0, 2.0)}
    factors = {'L0_attn_W_in': 8.0,
     'L0_attn_W_delta': 8.0,
     'L0_attn_b_delta': 8.0,
     'L0_attn_W_B': 8.0,
     'L0_attn_W_C': 8.0,
     'L0_attn_A_log': 8.0,
     'L0_attn_W_out': 8.0,
     'L0_ffn_Wg': 37.81,
     'L0_ffn_W1': 35.015,
     'L0_ffn_W2': 31.429,
     'L0_ffn_W3': 31.298,
     'L0_ffn_Ws1': 39.49,
     'L0_ffn_Ws2': 38.112,
     'L0_ffn_Ws3': 35.633}
    for name, (base, spread) in spreads.items():
        noise = np.random.default_rng([zlib.crc32(name.encode()), seed]).standard_normal(out[name].shape)
        drawn = base * np.exp(spread * noise) if base else spread * noise
        out[name] = jnp.asarray(drawn.astype(out[name].dtype))
    for name, factor in factors.items():
        out[name] = (out[name] * factor).astype(out[name].dtype)
    return out
```

```python
import concourse.bass as bass
from concourse import mybir
from contextlib import ExitStack

F32 = mybir.dt.float32
F32R = mybir.dt.float32r
BF16 = mybir.dt.bfloat16
ALU = mybir.AluOpType
ACT = mybir.ActivationFunctionType
AX = mybir.AxisListType

P = 128
SEQ = 256
TOK = 512
TT = TOK // P
DI = 256
NH = DI // P
NS = 16
GN = 2
NG = NS // GN
NU = NG * NH
E = 8
TOPK = 4
HID = 341
TILES = [128, 128, 85]
NX = E + 1
NK = 3 * NX
EPS = 1e-5

DA_RING = 8
HB_RING = 4
BB_RING = 4
ACT_RING = 9
GATE_STEPS = 13

BURSTS = [(-0.9, range(0, 4)), (5.0, range(4, 10)), (13.0, range(10, 16))]
GROUP_AT = [0.3, 2.6, 5.6, 8.1, 10.6, 13.6, 16.2, 18.8]


def timetables():
    pe, act, dve, pool = [], [], [], []

    def side(at, part, step, arg, reader):
        pe.append((at, part, step, arg))
        reader.append((at + 0.04, part, step, arg))

    side(-6.0, "e", "x1T", 0, act)
    side(-5.9, "m", "dz", 0, dve)
    side(-5.8, "m", "dz", 1, dve)
    side(-5.7, "m", "bc", 0, dve)
    side(-5.4, "e", "gate", 0, dve)
    side(-5.2, "m", "bT", 0, act)
    side(-0.5, "e", "wT", 0, act)
    act += [(-5.3, "m", "softplus", 0), (-0.6, "e", "gate_exp", 0)]
    dve += [(-5.5, "m", "delta", 0), (-0.55, "e", "gate_w", 0)]
    pool += [(-6.2, "e", "xsplit", 0), (-6.1, "m", "bsplit", 0), (-6.0, "m", "du", 0), (-0.52, "e", "wsplit", 0),
             (0.2, "e", "x1k", 0), (0.3, "m", "xcur", 0)]
    for at, units in BURSTS:
        act += [(at + 0.01 * i, "m", "decay", u) for i, u in enumerate(units)]
    for g, at in enumerate(GROUP_AT):
        for i in range(GN):
            side(at - 3.0 + 0.3 * i if g > 1 else -4.0 + 1.5 * g + 0.3 * i, "m", "bb", GN * g + i, act)
        for h in range(NH):
            pool.append((at - 2.2 + 0.8 * h if g > 1 else -3.0 + g + 0.1 * h, "m", "dbu", NH * g + h))
            dve.append((at + 0.5 * h, "m", "scan", NH * g + h))
        for i in range(2 * GN):
            pe.append((at + 0.8 + 0.6 * i, "m", "turn", 2 * GN * g + i))
            dve.append((at + 1.2 + 0.6 * i, "m", "sum", 2 * GN * g + i))
    end = GROUP_AT[-1] + 1.2 + 0.6 * 2 * GN
    side(end + 0.1, "m", "yT", 0, dve)
    side(end + 0.3, "m", "yT", 1, dve)
    side(end + 1.5, "m", "wo", 0, dve)
    dve += [(end + 2.2, "m", "x1n", 0)]
    pool += [(end + 0.2, "m", "y3", 0), (end + 0.5, "m", "y3", 1), (end + 1.8, "m", "rstd1", 0)]
    dve += [(19.0, "f", "ln", 0), (20.5, "f", "xn", 0)]
    pool += [(20.0, "f", "rstd", 0)]
    side(end + 0.6, "f", "xT", 0, act)
    for i in range(4):
        side(end + 1.0 + 0.71 * i, "f", "wi", i, act)
    for k in range(NK):
        x, c = divmod(k, 3)
        pe.append((k, "e", "h12", k))
        act.append((k + 0.05, "e", "silu", k))
        dve.append((k + 0.1, "e", "gated", k))
        w3_at = 5.01 + 0.01 * k if k < 5 else 13.01 + 0.05 * (k - 5) if k < 13 else k + 2.3
        pe.append((w3_at, "e", "w3", k))
        if c == 2:
            dve.append((w3_at + 0.01 if w3_at < 15 else w3_at + 0.3, "e", "eo", x))
            if x:
                pool.append((w3_at + 0.02 if w3_at < 15 else w3_at + 0.4, "e", "add", x))
                side({1: 10.9, 2: 11.9}.get(x, w3_at - 1.25 if x > 3 else 13.2), "e", "wb", x - 1, act)
    side(NK + 3.0, "e", "outT", 0, dve)
    return {n: sorted(v, key=lambda s: s[0]) for n, v in (("pe", pe), ("act", act), ("dve", dve), ("pool", pool))}


def mamba_moe_kernel(nc, x, w_in, w_delta, b_delta, w_b, w_c, a_log, d_param, w_out, wg_t, bias, w1_t, w2_t,
                     ws1_t, ws2_t, w3_t, ws3_t, out):
    NT = x.shape[0] * x.shape[1] // TOK
    steps = timetables()
    SIDE_PART = {"xT": "f", "wi": "f", "dz": "m", "bc": "m", "bT": "m", "bb": "m", "yT": "m", "wo": "m",
                 "x1T": "e", "gate": "e", "wT": "e", "wb": "e", "outT": "e"}

    def body_parts(j):
        return ("m" if j < NT else "") + ("e" if j > 0 else "") + ("f" if j + 1 < NT else "")

    def side_uses(parts):
        return [(s, a) for _, p, s, a in steps["pe"] if s in SIDE_PART and p in parts]

    FRONT = None
    FIRST = [("xT", 0)] + [("wi", i) for i in range(4)]

    def side_before(j):
        if isinstance(j, int):
            return len(FIRST) + sum(len(side_uses(body_parts(i))) for i in range(j))
        per = len(side_uses("mef"))
        return per * j + (side_before(2) - 2 * per)

    ctx = ExitStack()
    with ctx:
        def sb(name, shape, dt=F32):
            return ctx.enter_context(nc.sbuf_tensor(name, shape, dt))

        def bank(name):
            return ctx.enter_context(nc.psum_tensor(name, [P, 512], F32))

        def sem(name):
            return ctx.enter_context(nc.semaphore(name))

        ident = sb("ident", [P, P])
        ident_bf = sb("ident_bf", [P, P], BF16)
        sel_b = sb("sel_b", [3 * NS, NS, P], BF16)
        sel_w = sb("sel_w", [3 * E, E, P], BF16)
        before = sb("before", [P, E, E])
        half_exp = sb("half_exp", [P, TT])
        w_in_sb = sb("w_in_sb", [P, 2 * DI])
        w_delta_sb = sb("w_delta_sb", [P, NH, DI])
        w_bc_sb = sb("w_bc_sb", [P, NH, 2 * NS])
        w_out_sb = sb("w_out_sb", [P, NH, P])
        a_sb = sb("a_sb", [P, NH, NS])
        a_exp = sb("a_exp", [P, NH, NS])
        bd_sb = sb("bd_sb", [P, NH])
        dp_sb = sb("dp_sb", [P, NH])
        wg_sb = sb("wg_sb", [P, E])
        bias_sb = sb("bias_sb", [P, E])
        w1h = sb("w1h", [P, NX, HID], F32R)
        w1l = sb("w1l", [P, NX, HID], F32R)
        w2h = sb("w2h", [P, NX, HID], F32R)
        w2l = sb("w2l", [P, NX, HID], F32R)
        w3_sb = sb("w3_sb", [P, NX, 3, P])
        x_in = sb("x_in", [P, TT, P])
        x_cur = sb("x_cur", [P, TT, P])
        xn = sb("xn", [P, TT, P])
        xnT = sb("xnT", [P, TOK])
        u = sb("u", [P, NH, TOK])
        sres = sb("sres", [P, NH, TOK])
        delta = sb("delta", [P, NH, TOK])
        sp = sb("sp", [P, NH, TOK])
        du = sb("du", [P, NH, TOK])
        bc = sb("bc", [P, TT, 2 * NS])
        bparts = sb("bparts", [P, TT, 3, NS], BF16)
        brest = sb("brest", [P, 2, TT, NS])
        bT = sb("bT", [3 * NS, TOK], BF16)
        bbc = sb("bbc", [P, BB_RING, TOK])
        decay = sb("decay", [P, DA_RING, GN, TOK])
        hb = sb("hb", [P, HB_RING, GN, TOK])
        acc = sb("acc", [P, TT, DI])
        one = sb("one", [P, 1])
        ln_one = sb("ln_one", [P, 1])
        stats = {t: sb(f"stats_{t}", [P, TT, 6]) for t in ("x", "x1")}
        mv = {t: sb(f"mv_{t}", [P, TT, 2]) for t in ("x", "x1")}
        veps = {t: sb(f"veps_{t}", [P, TT]) for t in ("x", "x1")}
        rstd = {t: sb(f"rstd_{t}", [P, TT]) for t in ("x", "x1")}
        x1 = sb("x1", [P, TT, P])
        x1k = sb("x1k", [P, TT, P])
        x1n = xn
        x1nT = sb("x1nT", [P, TOK])
        xh = sb("xh", [P, TOK], F32R)
        xl = sb("xl", [P, TOK], F32R)
        g = sb("g", [P, TT, E])
        eo_w = sb("eo_w", [P, 2, TOK])
        cmp_gt, cmp_ge = (eo_w[:, i, 0:TT * E * E].rearrange("p (t e j) -> p t e j", t=TT, e=E) for i in range(2))
        rank = sb("rank", [P, TT, E])
        mask = sb("mask", [P, TT, E])
        gmax = sb("gmax", [P, TT])
        gm = sb("gm", [P, TT, E])
        gex = sb("gex", [P, TT, E])
        gem = sb("gem", [P, TT, E])
        gsum = sb("gsum", [P, TT])
        ginv = sb("ginv", [P, TT])
        w = sb("w", [P, TT, E])
        wparts = sb("wparts", [P, TT, 3, E], BF16)
        wrest = sb("wrest", [P, 2, TT, E])
        wT = sb("wT", [3 * E, TOK], BF16)
        wbc = sb("wbc", [P, 2, TOK])
        s = sb("s", [P, 2, TOK])
        gated = sb("gated", [P, ACT_RING, TOK])
        stage = gated[:, :, :].rearrange("p a t -> p (a t)")[:, 0:NX * HID]
        moe = x1nT

        h1_bank = [bank(f"h1_{i}") for i in range(2)]
        h2_bank = [bank(f"h2_{i}") for i in range(2)]
        eo_bank = bank("eo_bank")
        turn_bank = [bank(f"turn_{i}") for i in range(2)]
        side = bank("side")
        side_bf = side[:, :].bitcast(BF16)

        consts = sem("consts")
        small_in = sem("small_in")
        w1_in, w2_in, w3_in = sem("w1_in"), sem("w2_in"), sem("w3_in")
        a_exped, a_ready = sem("a_exped"), sem("a_ready")
        w_hi, w_lo = sem("w_hi"), sem("w_lo")
        x_in_sem, out_stored = sem("x_in_sem"), sem("out_stored")
        ln_steps = {"x": sem("ln_steps_x"), "x1": sem("ln_steps_x1")}
        rstd_steps = {"x": sem("rstd_steps_x"), "x1": sem("rstd_steps_x1")}
        xn_ready = {"x": sem("xn_ready_x"), "x1": sem("xn_ready_x1")}
        x_cur_ready = sem("x_cur_ready")
        xnT_ready, wi_ready = sem("xnT_ready"), sem("wi_ready")
        side_full = sem("side_full")
        zb_ready, sp_steps, delta_ready, du_ready = sem("zb_ready"), sem("sp_steps"), sem("delta_ready"), sem("du_ready")
        bc_ready, bparts_steps, bT_ready, bb_ready = sem("bc_ready"), sem("bparts_steps"), sem("bT_ready"), sem("bb_ready")
        dbu_ready, decay_ready, scanned = sem("dbu_ready"), sem("decay_ready"), sem("scanned")
        turned, summed = sem("turned"), sem("summed")
        y2_ready, y3_ready = sem("y2_ready"), sem("y3_ready")
        x1_ready, x1k_ready, x1T_ready, xsplit = sem("x1_ready"), sem("x1k_ready"), sem("x1T_ready"), sem("xsplit")
        gate_steps, gex_ready, wparts_steps, wT_ready, wbc_ready = (
            sem("gate_steps"), sem("gex_ready"), sem("wparts_steps"), sem("wT_ready"), sem("wbc_ready"))
        h1_full, h2_full, s_ready, gated_ready = sem("h1_full"), sem("h2_full"), sem("s_ready"), sem("gated_ready")
        w3_done, eo_done, added, out_ready = sem("w3_done"), sem("eo_done"), sem("added"), sem("out_ready")
        ln_primed = sem("ln_primed")

        x_t = x.rearrange("b (c p) d -> p (b c) d", p=P)
        out_t = out.rearrange("b (c p) d -> p (b c) d", p=P)

        def wait(eng, s_, turn, per, c):
            j, shift = turn
            value = per * j + (per * shift + c)
            if isinstance(value, int) and value <= 0:
                return
            eng.wait_ge(s_, value)

        def carry_waits(eng):
            eng.nop(nofuse=True)

        def bodies(eng, program):
            program(0, body_parts(0))
            program(1, body_parts(1))
            with eng.Fori(2, NT - 1) as j:
                program(j, "mef")
            program(NT - 1, body_parts(NT - 1))
            program(NT, body_parts(NT))

        def turns(j):
            return {"m": (j, 0), "e": (j, -1), "f": (j, 1)}

        def side_index(j, parts, step, arg):
            if j is FRONT:
                return FIRST.index((step, arg)) + 1
            return side_uses(parts).index((step, arg)) + 1 + side_before(j)

        def hidden_ring(k):
            return k - 2 if k >= 2 else (NK - 1 if k == 0 else NK - 2) - NK

        SMALL = 10
        CONSTS = 16
        block = ctx.enter_context(nc.Block())

        @block.sync
        def _(sp_eng):
            def load_x(turn):
                wait(sp_eng, xn_ready["x"], turn, TT, 0)
                carry_waits(sp_eng)
                wait(sp_eng, x_cur_ready, turn, 1, 0)
                j, shift = turn
                at = (j + shift) * TT if isinstance(j, int) else j * TT + shift * TT
                if shift:
                    carry_waits(sp_eng)
                sp_eng.dma_start(x_in[:, :, :], x_t[:, bass.ds(at, TT), :]).then_inc(x_in_sem, 16)

            load_x((0, 0))
            small = [(w_in_sb[:, :], w_in), (w_delta_sb[:, :, :], w_delta.rearrange("(k p) n -> p k n", p=P)),
                     (w_bc_sb[:, :, 0:NS], w_b.rearrange("(k p) n -> p k n", p=P)),
                     (w_bc_sb[:, :, NS:], w_c.rearrange("(k p) n -> p k n", p=P)),
                     (w_out_sb[:, :, :], w_out.rearrange("(k p) n -> p k n", p=P)),
                     (a_sb[:, :, :], a_log.rearrange("(k p) n -> p k n", p=P)),
                     (bd_sb[:, :], b_delta),
                     (dp_sb[:, :], d_param),
                     (wg_sb[:, :], wg_t), (bias_sb[:, :], bias.partition_broadcast(P))]
            for dst, src in small:
                sp_eng.dma_start(dst, src).then_inc(small_in, 16)
            assert len(small) == SMALL
            sp_eng.dma_start(stage[:, 0:HID], ws1_t).then_inc(w1_in, 16)
            sp_eng.dma_start(stage[:, HID:].rearrange("p (e h) -> p e h", e=E), w1_t).then_inc(w1_in, 16)
            for c, rows in enumerate(TILES):
                sp_eng.dma_start(w3_sb[0:rows, 0, c, :], ws3_t[P * c:P * c + rows, :]).then_inc(w3_in, 16)
                sp_eng.dma_start(w3_sb[0:rows, 1:, c, :],
                                 w3_t[:, P * c:P * c + rows, :].rearrange("e h d -> h e d")).then_inc(w3_in, 16)
            sp_eng.wait_ge(w_lo, 1)
            sp_eng.dma_start(stage[:, 0:HID], ws2_t).then_inc(w2_in, 16)
            sp_eng.dma_start(stage[:, HID:].rearrange("p (e h) -> p e h", e=E), w2_t).then_inc(w2_in, 16)

            def program(j, parts):
                t = turns(j)
                if "f" in parts:
                    load_x(t["f"])
                if "e" in parts:
                    wait(sp_eng, out_ready, t["e"], 1, 1)
                    at = (j - 1) * TT if isinstance(j, int) else j * TT - TT
                    carry_waits(sp_eng)
                    sp_eng.dma_start(out_t[:, bass.ds(at, TT), :], x1k[:, :, :]).then_inc(out_stored, 16)

            bodies(sp_eng, program)
            sp_eng.wait_ge(out_stored, 16 * NT)

        @block.gpsimd
        def _(pool):
            pool.memset(ident[:, :], 0.0).then_inc(consts, 1)
            pool.memset(sel_b[:, :, :], 0.0).then_inc(consts, 1)
            pool.memset(sel_w[:, :, :], 0.0).then_inc(consts, 1)
            pool.memset(before[:, :, :], 1.0).then_inc(consts, 1)
            pool.wait_ge(consts, 4)
            pool.affine_select(out=ident[:, :], in_=ident[:, :], compare_op=ALU.not_equal, fill=1.0, base=0,
                               pattern=[[-1, P]], channel_multiplier=1).then_inc(consts, 1)
            pool.affine_select(out=before[:, :, :], in_=before[:, :, :], compare_op=ALU.is_ge, fill=0.0, base=-1,
                               pattern=[[1, E], [-1, E]], channel_multiplier=0).then_inc(consts, 1)
            for i in range(3):
                pool.wait_ge(consts, 6 + 2 * i)
                pool.affine_select(out=sel_b[:, :, :], in_=sel_b[:, :, :], compare_op=ALU.not_equal, fill=1.0,
                                   base=-NS * i, pattern=[[-1, NS], [0, P]], channel_multiplier=1).then_inc(consts, 1)
                pool.affine_select(out=sel_w[:, :, :], in_=sel_w[:, :, :], compare_op=ALU.not_equal, fill=1.0,
                                   base=-E * i, pattern=[[-1, E], [0, P]], channel_multiplier=1).then_inc(consts, 1)
            pool.tensor_copy(ident_bf[:, :], ident[:, :]).then_inc(consts, 1)
            pool.memset(half_exp[:, :], -0.5).then_inc(consts, 1)
            pool.memset(one[:, :], 1.0).then_inc(consts, 1)
            pool.memset(decay[:, :, :, :].rearrange("p r n (b t) -> p (r n b) t", t=SEQ)[:, :, 0:1], 0.0).then_inc(consts, 1)

            def take_rstd(norm, turn):
                wait(pool, ln_steps[norm], turn, 2 * TT, 2 * TT)
                wait(pool, xn_ready[norm], turn, TT, 0)
                carry_waits(pool)
                pool.tensor_scalar(veps[norm][:, :], mv[norm][:, :, 1], EPS, 1.0, ALU.add, ALU.mult)\
                    .then_inc(rstd_steps[norm], 1)
                wait(pool, rstd_steps[norm], turn, 2, 1)
                pool.tensor_tensor(rstd[norm][:, :], veps[norm][:, :], half_exp[:, :], ALU.pow)\
                    .then_inc(rstd_steps[norm], 1)

            def cut(parts_tile, rest, src, steps_sem, turn):
                for i in range(3):
                    cur = src if i == 0 else rest[:, i - 1]
                    if i:
                        wait(pool, steps_sem, turn, 5, 2 * i)
                    carry_waits(pool)
                    pool.tensor_copy(parts_tile[:, :, i, :], cur).then_inc(steps_sem, 1)
                    if i < 2:
                        wait(pool, steps_sem, turn, 5, 2 * i + 1)
                        pool.tensor_tensor(rest[:, i], cur, parts_tile[:, :, i, :], ALU.subtract)\
                            .then_inc(steps_sem, 1)

            def program(j, parts):
                t = turns(j)
                m, e, f = t["m"], t["e"], t["f"]
                for _, part, step, arg in steps["pool"]:
                    if part not in parts:
                        continue
                    if step == "xsplit":
                        wait(pool, x1T_ready, e, 1, 1)
                        wait(pool, h2_full, e, NK, 0)
                        carry_waits(pool)
                        pool.tensor_copy(xh[:, :], x1nT[:, :]).then_inc(xsplit, 1)
                        wait(pool, xsplit, e, 2, 1)
                        pool.tensor_tensor(xl[:, :], x1nT[:, :], xh[:, :].bitcast(F32), ALU.subtract).then_inc(xsplit, 1)
                    elif step == "bsplit":
                        wait(pool, bc_ready, m, 1, 1)
                        wait(pool, bT_ready, m, 1, 0)
                        cut(bparts, brest, bc[:, :, 0:NS], bparts_steps, m)
                    elif step == "du":
                        wait(pool, delta_ready, m, 1, 1)
                        wait(pool, dbu_ready, m, NU, 0)
                        pool.tensor_tensor(du[:, :, :], delta[:, :, :], u[:, :, :], ALU.mult).then_inc(du_ready, 1)
                    elif step == "dbu":
                        grp, h = divmod(arg, NH)
                        wait(pool, du_ready, m, 1, 1)
                        wait(pool, bb_ready, m, NS, GN * grp + GN)
                        wait(pool, turned, m, 2 * NS, 2 * GN * (grp - HB_RING // NH + 1))
                        r = GN * grp % BB_RING
                        pool.tensor_tensor(hb[:, arg % HB_RING, :, :],
                                           du[:, h, :].unsqueeze(1).broadcast_to((P, GN, TOK)),
                                           bbc[:, r:r + GN, :], ALU.mult).then_inc(dbu_ready, 1)
                    elif step == "y3":
                        wait(pool, y2_ready, m, NH, arg + 1)
                        pool.tensor_tensor(sp[:, arg, :], sp[:, arg, :], sres[:, arg, :], ALU.mult).then_inc(y3_ready, 1)
                    elif step == "rstd1":
                        take_rstd("x1", m)
                    elif step == "rstd":
                        take_rstd("x", f)
                    elif step == "wsplit":
                        wait(pool, gate_steps, e, GATE_STEPS, GATE_STEPS)
                        wait(pool, wT_ready, e, 1, 0)
                        cut(wparts, wrest, w[:, :, :], wparts_steps, e)
                    elif step == "x1k":
                        wait(pool, x1_ready, e, 1, 1)
                        wait(pool, out_stored, e, 16, 0)
                        carry_waits(pool)
                        pool.tensor_copy(x1k[:, :, :], x1[:, :, :]).then_inc(x1k_ready, 1)
                    elif step == "xcur":
                        wait(pool, x_in_sem, m, 16, 16)
                        wait(pool, x1_ready, m, 1, 0)
                        carry_waits(pool)
                        pool.tensor_copy(x_cur[:, :, :], x_in[:, :, :]).then_inc(x_cur_ready, 1)
                    elif step == "add":
                        wait(pool, eo_done, e, NX, arg + 1)
                        wait(pool, added, e, E, arg - 1)
                        pool.tensor_tensor(moe[:, :], moe[:, :], eo_w[:, arg % 2, :], ALU.add).then_inc(added, 1)

            take_rstd("x", (0, 0))
            bodies(pool, program)

        @block.scalar
        def _(act):
            def read_side(j, parts, step, arg, out_ap, in_ap, func, ready):
                act.wait_ge(side_full, side_index(j, parts, step, arg))
                act.activation(out_ap, in_ap, func).then_inc(ready, 1)

            def project_in(j, parts, f, step, arg):
                if step == "xT":
                    read_side(j, parts, "xT", 0, xnT[:, :], side[:, :], ACT.Copy, xnT_ready)
                else:
                    if arg < NH:
                        wait(act, y2_ready, f, NH, 0)
                    else:
                        wait(act, y3_ready, f, NH, 0)
                    dst = u if arg < NH else sres
                    read_side(j, parts, "wi", arg, dst[:, arg % NH, :], side[:, :], ACT.Silu, wi_ready)

            def program(j, parts):
                t = turns(j)
                m, e, f = t["m"], t["e"], t["f"]
                for _, part, step, arg in steps["act"]:
                    if part not in parts:
                        continue
                    if step == "x1T":
                        wait(act, xsplit, e, 2, 0)
                        wait(act, gate_steps, e, GATE_STEPS, 0)
                        read_side(j, parts, step, arg, x1nT[:, :], side[:, :], ACT.Copy, x1T_ready)
                    elif step == "softplus":
                        wait(act, ln_primed, m, 1, 0)
                        act.activation(ln_one[:, :], one[:, :], ACT.Ln).then_inc(ln_primed, 1)
                        wait(act, zb_ready, m, NH, NH)
                        wait(act, x1_ready, m, 1, 0)
                        act.activation(sp[:, :, :], delta[:, :, :], ACT.Abs).then_inc(sp_steps, 1)
                        wait(act, sp_steps, m, 3, 1)
                        act.activation(sp[:, :, :], sp[:, :, :], ACT.Exp, scale=-1.0).then_inc(sp_steps, 1)
                        wait(act, sp_steps, m, 3, 2)
                        act.activation(sp[:, :, :], sp[:, :, :], ACT.Ln, bias=one[:, :]).then_inc(sp_steps, 1)
                    elif step == "bT":
                        read_side(j, parts, step, arg, bT[:, :], side_bf[0:3 * NS, 0:TOK], ACT.Copy, bT_ready)
                    elif step == "bb":
                        wait(act, dbu_ready, m, NU, NH * ((arg - BB_RING) // GN + 1))
                        read_side(j, parts, step, arg, bbc[:, arg % BB_RING, :], side[:, :], ACT.Copy, bb_ready)
                    elif step == "decay":
                        grp, h = divmod(arg, NH)
                        wait(act, delta_ready, m, 1, 1)
                        wait(act, scanned, m, NU, arg - DA_RING + 1)
                        for i in range(GN):
                            act.activation(
                                decay[:, arg % DA_RING, i, :].rearrange("p (b t) -> p b t", t=SEQ)[:, :, 1:],
                                delta[:, h, :].rearrange("p (b t) -> p b t", t=SEQ)[:, :, 1:],
                                ACT.Exp, scale=a_sb[:, h, GN * grp + i:GN * grp + i + 1]).then_inc(decay_ready, 1)
                    elif step == "gate_exp":
                        wait(act, gate_steps, e, GATE_STEPS, 9)
                        act.activation(gex[:, :, :], gm[:, :, :], ACT.Exp).then_inc(gex_ready, 1)
                    elif step == "wT":
                        read_side(j, parts, step, arg, wT[:, :], side_bf[0:3 * E, 0:TOK], ACT.Copy, wT_ready)
                    elif step == "wb":
                        wait(act, eo_done, e, NX, arg)
                        read_side(j, parts, step, arg, wbc[:, arg % 2, :], side[:, :], ACT.Copy, wbc_ready)
                    elif step == "silu":
                        rows = TILES[arg % 3]
                        wait(act, h1_full, e, NK, arg + 1)
                        wait(act, gated_ready, e, NK, hidden_ring(arg) + 1)
                        act.activation(s[0:rows, arg % 2, :], h1_bank[arg % 2][0:rows, :], ACT.Silu)\
                           .then_inc(s_ready, 1)
                    else:
                        project_in(j, parts, f, step, arg)
                    if isinstance(j, int) and j == 0 and step == "decay" and arg in (3, 9):
                        cut_hi(arg == 9)

            def cut_hi(second):
                act.wait_ge(w2_in if second else w1_in, 32)
                dst = w2h if second else w1h
                act.activation(dst[:, :, :].rearrange("p x h -> p (x h)"), stage, ACT.Copy).then_inc(w_hi, 1)

            act.wait_ge(small_in, 16 * SMALL)
            act.activation(a_exp[:, :, :], a_sb[:, :, :], ACT.Exp).then_inc(a_exped, 1)
            act.wait_ge(consts, CONSTS)
            for step, arg in FIRST:
                project_in(FRONT, "", (0, 0), step, arg)
            act.wait_ge(a_ready, 1)
            bodies(act, program)

        @block.vector
        def _(dve):
            def take_stats(norm, src, turn):
                for i in range(TT):
                    dve.bn_stats(stats[norm][:, i, :], src[:, i, :]).then_inc(ln_steps[norm], 1)
                for i in range(TT):
                    wait(dve, ln_steps[norm], turn, 2 * TT, i + 1)
                    carry_waits(dve)
                    dve.bn_aggr(mv[norm][:, i, :], stats[norm][:, i, :]).then_inc(ln_steps[norm], 1)

            def normalize(norm, src, dst, turn):
                wait(dve, rstd_steps[norm], turn, 2, 2)
                for i in range(TT):
                    dve.tensor_scalar(dst[:, i, :], src[:, i, :], mv[norm][:, i, 0:1], rstd[norm][:, i:i + 1],
                                      ALU.subtract, ALU.mult).then_inc(xn_ready[norm], 1)

            def layer_in(f, step):
                if step == "ln":
                    wait(dve, x_in_sem, f, 16, 16)
                    take_stats("x", x_in, f)
                else:
                    wait(dve, x1T_ready, f, 1, -1)
                    normalize("x", x_in, xn, f)

            def side_wait(j, parts, step, arg):
                dve.wait_ge(side_full, side_index(j, parts, step, arg))

            def cut_lo(second):
                dve.wait_ge(w_hi, 2 if second else 1)
                hi, lo = (w2h, w2l) if second else (w1h, w1l)
                dve.tensor_tensor(lo[:, :, :].rearrange("p x h -> p (x h)"), stage,
                                  hi[:, :, :].rearrange("p x h -> p (x h)").bitcast(F32), ALU.subtract).then_inc(w_lo, 1)

            def program(j, parts):
                t = turns(j)
                m, e, f = t["m"], t["e"], t["f"]
                for _, part, step, arg in steps["dve"]:
                    if part not in parts:
                        continue
                    if step == "dz":
                        wait(dve, decay_ready, m, NS * NH, 0)
                        wait(dve, du_ready, m, 1, 0)
                        side_wait(j, parts, "dz", arg)
                        dve.tensor_scalar(delta[:, arg, :], side[:, :], bd_sb[:, arg:arg + 1], None, ALU.add)\
                           .then_inc(zb_ready, 1)
                    elif step == "bc":
                        wait(dve, bparts_steps, m, 5, 0)
                        wait(dve, summed, m, NS * TT, 0)
                        side_wait(j, parts, "bc", 0)
                        dve.tensor_copy(bc[:, :, :], side[:, 0:TT * 2 * NS].rearrange("p (t n) -> p t n", t=TT))\
                           .then_inc(bc_ready, 1)
                    elif step == "delta":
                        wait(dve, sp_steps, m, 3, 3)
                        dve.scalar_tensor_tensor(delta[:, :, :], delta[:, :, :], 0.0, sp[:, :, :], ALU.max, ALU.add)\
                           .then_inc(delta_ready, 1)
                    elif step == "scan":
                        wait(dve, decay_ready, m, NS * NH, GN * (arg + 1))
                        wait(dve, dbu_ready, m, NU, arg + 1)
                        states = hb[:, arg % HB_RING, :, :].rearrange("p n t -> p (n t)")
                        dve.tensor_tensor_scan(states,
                                               decay[:, arg % DA_RING, :, :].rearrange("p n t -> p (n t)"),
                                               states, 0.0, ALU.mult, ALU.add).then_inc(scanned, 1)
                    elif step == "sum":
                        n, pair = divmod(arg, 2)
                        wait(dve, turned, m, 2 * NS, arg + 1)
                        if n:
                            wait(dve, summed, m, NS * TT, 2 * arg - 2)
                        else:
                            wait(dve, bc_ready, m, 1, 1)
                        for i in range(2):
                            blk = 2 * pair + i
                            hT = turn_bank[pair][:, i * DI:(i + 1) * DI]
                            c_n = bc[:, blk, NS + n:NS + n + 1]
                            if n:
                                ins = dve.scalar_tensor_tensor(acc[:, blk, :], hT, c_n, acc[:, blk, :], ALU.mult, ALU.add)
                            else:
                                ins = dve.tensor_scalar(acc[:, blk, :], hT, c_n, None, ALU.mult)
                            ins.then_inc(summed, 1)
                    elif step == "yT":
                        side_wait(j, parts, "yT", arg)
                        dve.scalar_tensor_tensor(sp[:, arg, :], u[:, arg, :], dp_sb[:, arg:arg + 1], side[:, :],
                                                 ALU.mult, ALU.add).then_inc(y2_ready, 1)
                    elif step == "wo":
                        wait(dve, x_cur_ready, m, 1, 1)
                        wait(dve, x1k_ready, m, 1, 0)
                        wait(dve, xn_ready["x1"], m, TT, 0)
                        side_wait(j, parts, "wo", 0)
                        dve.tensor_tensor(x1[:, :, :], side[:, :].rearrange("p (t d) -> p t d", t=TT), x_cur[:, :, :],
                                          ALU.add).then_inc(x1_ready, 1)
                        wait(dve, x1_ready, m, 1, 1)
                        take_stats("x1", x1, m)
                    elif step == "x1n":
                        if "f" in parts:
                            wait(dve, xnT_ready, f, 1, 1)
                        normalize("x1", x1, x1n, m)
                    elif step == "gate":
                        def then(c, ins):
                            ins.then_inc(gate_steps, 1)
                            wait(dve, gate_steps, e, GATE_STEPS, c)

                        wait(dve, added, e, E, 0)
                        side_wait(j, parts, "gate", 0)
                        then(1, dve.tensor_tensor(g[:, :, :], side[:, 0:TT * E].rearrange("p (t e) -> p t e", t=TT),
                                                  bias_sb[:, :].unsqueeze(1).broadcast_to((P, TT, E)), ALU.add))
                        gj = g[:, :, :].unsqueeze(2).broadcast_to((P, TT, E, E))
                        ge = g[:, :, :].unsqueeze(3).broadcast_to((P, TT, E, E))
                        then(2, dve.tensor_tensor(cmp_gt[:, :, :, :], gj, ge, ALU.is_gt))
                        then(3, dve.tensor_tensor(cmp_ge[:, :, :, :], gj, ge, ALU.is_ge))
                        then(4, dve.tensor_tensor(cmp_ge[:, :, :, :], cmp_ge[:, :, :, :],
                                                  before[:, :, :].unsqueeze(1).broadcast_to((P, TT, E, E)), ALU.mult))
                        then(5, dve.tensor_tensor(cmp_gt[:, :, :, :], cmp_gt[:, :, :, :], cmp_ge[:, :, :, :], ALU.max))
                        then(6, dve.tensor_reduce(rank[:, :, :], cmp_gt[:, :, :, :], AX.X, ALU.add))
                        then(7, dve.tensor_scalar(mask[:, :, :], rank[:, :, :], TOPK - 0.5, None, ALU.is_lt))
                        then(8, dve.tensor_reduce(gmax[:, :], g[:, :, :], AX.X, ALU.max))
                        then(9, dve.tensor_tensor(gm[:, :, :], g[:, :, :],
                                                  gmax[:, :].unsqueeze(2).broadcast_to((P, TT, E)), ALU.subtract))
                    elif step == "gate_w":
                        def then(c, ins):
                            ins.then_inc(gate_steps, 1)
                            wait(dve, gate_steps, e, GATE_STEPS, c)

                        wait(dve, gex_ready, e, 1, 1)
                        wait(dve, wparts_steps, e, 5, 0)
                        then(10, dve.tensor_tensor(gem[:, :, :], gex[:, :, :], mask[:, :, :], ALU.mult))
                        then(11, dve.tensor_reduce(gsum[:, :], gem[:, :, :], AX.X, ALU.add))
                        then(12, dve.reciprocal(ginv[:, :], gsum[:, :]))
                        then(13, dve.tensor_tensor(w[:, :, :], gem[:, :, :],
                                                   ginv[:, :].unsqueeze(2).broadcast_to((P, TT, E)), ALU.mult))
                    elif step == "gated":
                        rows = TILES[arg % 3]
                        wait(dve, h2_full, e, NK, arg + 1)
                        wait(dve, s_ready, e, NK, arg + 1)
                        wait(dve, w3_done, e, NK, arg - ACT_RING + 1)
                        dve.tensor_tensor(gated[0:rows, arg % ACT_RING, :], h2_bank[arg % 2][0:rows, :],
                                          s[0:rows, arg % 2, :], ALU.mult).then_inc(gated_ready, 1)
                    elif step == "eo":
                        wait(dve, w3_done, e, NK, 3 * arg + 3)
                        if arg == 0:
                            dve.tensor_copy(moe[:, :], eo_bank[:, :]).then_inc(eo_done, 1)
                        else:
                            wait(dve, wbc_ready, e, E, arg)
                            wait(dve, added, e, E, arg - 2)
                            dve.tensor_tensor(eo_w[:, arg % 2, :], eo_bank[:, :], wbc[:, (arg - 1) % 2, :], ALU.mult)\
                               .then_inc(eo_done, 1)
                    elif step == "outT":
                        wait(dve, x1k_ready, e, 1, 1)
                        side_wait(j, parts, "outT", 0)
                        dve.tensor_tensor(x1k[:, :, :], side[:, :].rearrange("p (t d) -> p t d", t=TT), x1k[:, :, :],
                                          ALU.add).then_inc(out_ready, 1)
                    else:
                        layer_in(f, step)
                    if isinstance(j, int) and j == 0 and step == "scan" and arg in (3, 9):
                        cut_lo(arg == 9)

            layer_in((0, 0), "ln")
            layer_in((0, 0), "xn")
            dve.wait_ge(a_exped, 1)
            dve.tensor_scalar(a_sb[:, :, :], a_exp[:, :, :], -1.0, None, ALU.mult).then_inc(a_ready, 1)
            dve.wait_ge(small_in, 16 * SMALL)
            dve.wait_ge(consts, CONSTS)
            bodies(dve, program)

        @block.tensor
        def _(pe):
            SIDE_READ = {"xT": (xnT_ready, 1), "wi": (wi_ready, 4), "dz": (zb_ready, NH), "bc": (bc_ready, 1),
                         "bT": (bT_ready, 1), "bb": (bb_ready, NS), "yT": (y2_ready, NH), "wo": (x1_ready, 1),
                         "x1T": (x1T_ready, 1), "gate": (gate_steps, GATE_STEPS), "wT": (wT_ready, 1),
                         "wb": (wbc_ready, E), "outT": (out_ready, 1)}

            def side_free(j, parts, step, arg):
                uses = FIRST if j is FRONT else side_uses(parts)
                n = uses.index((step, arg))
                if n == 0 and j is FRONT:
                    return
                if n:
                    before_it, turn = uses[n - 1], ((0, 0) if j is FRONT else turns(j)[SIDE_PART[uses[n - 1][0]]])
                elif isinstance(j, int) and j == 0:
                    before_it, turn = FIRST[-1], (0, 0)
                else:
                    last_parts = body_parts(j - 1) if isinstance(j, int) else "mef"
                    before_it = side_uses(last_parts)[-1]
                    turn = (j, turns(j)[SIDE_PART[before_it[0]]][1] - 1)
                reader, per = SIDE_READ[before_it[0]]
                wait(pe, reader, turn, per, before_it[1] + 1)

            def project_in(j, parts, f, step, arg):
                if step == "xT":
                    wait(pe, xn_ready["x"], f, TT, TT)
                    side_free(j, parts, step, arg)
                    for i in range(TT):
                        mm = pe.transpose(side[:, i * P:(i + 1) * P], xn[:, i, :], ident[:, :])
                else:
                    wait(pe, xnT_ready, f, 1, 1)
                    side_free(j, parts, step, arg)
                    mm = pe.matmul(side[:, :], w_in_sb[:, arg * P:(arg + 1) * P], xnT[:, :], start=True, stop=True)
                mm.then_inc(side_full, 1)

            def program(j, parts):
                t = turns(j)
                m, e, f = t["m"], t["e"], t["f"]
                for _, part, step, arg in steps["pe"]:
                    if part not in parts:
                        continue
                    if step == "x1T":
                        wait(pe, xn_ready["x1"], e, TT, TT)
                        side_free(j, parts, step, arg)
                        for i in range(TT):
                            mm = pe.transpose(side[:, i * P:(i + 1) * P], x1n[:, i, :], ident[:, :])
                        mm.then_inc(side_full, 1)
                    elif step == "dz":
                        wait(pe, wi_ready, m, 4, 4)
                        side_free(j, parts, step, arg)
                        for k in range(NH):
                            mm = pe.matmul(side[:, :], w_delta_sb[:, k, arg * P:(arg + 1) * P], u[:, k, :],
                                           start=(k == 0), stop=(k == NH - 1))
                        mm.then_inc(side_full, 1)
                    elif step == "bc":
                        side_free(j, parts, step, arg)
                        for i in range(TT):
                            for k in range(NH):
                                mm = pe.matmul(side[:, i * 2 * NS:(i + 1) * 2 * NS], u[:, k, i * P:(i + 1) * P],
                                               w_bc_sb[:, k, :], start=(k == 0), stop=(k == NH - 1))
                        mm.then_inc(side_full, 1)
                    elif step == "gate":
                        wait(pe, x1T_ready, e, 1, 1)
                        side_free(j, parts, step, arg)
                        for i in range(TT):
                            mm = pe.matmul(side[:, i * E:(i + 1) * E], x1nT[:, i * P:(i + 1) * P], wg_sb[:, :],
                                           start=True, stop=True)
                        mm.then_inc(side_full, 1)
                    elif step == "bT":
                        wait(pe, bparts_steps, m, 5, 5)
                        side_free(j, parts, step, arg)
                        carry_waits(pe)
                        for i in range(TT):
                            mm = pe.transpose(side_bf[0:3 * NS, i * P:(i + 1) * P],
                                              bparts[:, i, :, :].rearrange("p c n -> p (c n)"), ident_bf[:, :])
                        mm.then_inc(side_full, 1)
                    elif step == "bb":
                        wait(pe, bT_ready, m, 1, 1)
                        side_free(j, parts, step, arg)
                        pe.matmul(side[:, :], sel_b[:, arg, :], bT[:, :], start=True, stop=True).then_inc(side_full, 1)
                    elif step == "wT":
                        wait(pe, wparts_steps, e, 5, 5)
                        side_free(j, parts, step, arg)
                        carry_waits(pe)
                        for i in range(TT):
                            mm = pe.transpose(side_bf[0:3 * E, i * P:(i + 1) * P],
                                              wparts[:, i, :, :].rearrange("p c n -> p (c n)"), ident_bf[:, :])
                        mm.then_inc(side_full, 1)
                    elif step == "wb":
                        wait(pe, wT_ready, e, 1, 1)
                        side_free(j, parts, step, arg)
                        pe.matmul(side[:, :], sel_w[:, arg, :], wT[:, :], start=True, stop=True).then_inc(side_full, 1)
                    elif step == "turn":
                        n, pair = divmod(arg, 2)
                        grp, i_n = divmod(n, GN)
                        wait(pe, scanned, m, NU, NH * (grp + 1))
                        wait(pe, summed, m, NS * TT, 2 * arg - 2)
                        for i in range(2):
                            blk = 2 * pair + i
                            for h in range(NH):
                                mm = pe.transpose(turn_bank[pair][:, (NH * i + h) * P:(NH * i + h + 1) * P],
                                                  hb[:, (NH * grp + h) % HB_RING, i_n, blk * P:(blk + 1) * P],
                                                  ident[:, :])
                        mm.then_inc(turned, 1)
                    elif step == "yT":
                        wait(pe, summed, m, NS * TT, NS * TT)
                        side_free(j, parts, step, arg)
                        for i in range(TT):
                            mm = pe.transpose(side[:, i * P:(i + 1) * P], acc[:, i, arg * P:(arg + 1) * P], ident[:, :])
                        mm.then_inc(side_full, 1)
                    elif step == "wo":
                        wait(pe, y3_ready, m, NH, NH)
                        side_free(j, parts, step, arg)
                        for i in range(TT):
                            for k in range(NH):
                                mm = pe.matmul(side[:, i * P:(i + 1) * P], sp[:, k, i * P:(i + 1) * P], w_out_sb[:, k, :],
                                               start=(k == 0), stop=(k == NH - 1))
                        mm.then_inc(side_full, 1)
                    elif step == "h12":
                        xx, c = divmod(arg, 3)
                        rows = TILES[c]
                        cols = slice(c * P, c * P + rows)
                        if arg == 0:
                            wait(pe, xsplit, e, 2, 2)
                            if isinstance(j, int) and j == 1:
                                pe.wait_ge(w_lo, 2)
                        for banks, hi, lo, free, full in ((h1_bank, w1h, w1l, s_ready, h1_full),
                                                          (h2_bank, w2h, w2l, gated_ready, h2_full)):
                            wait(pe, free, e, NK, hidden_ring(arg) + 1)
                            dst = banks[arg % 2][0:rows, :]
                            pe.matmul(dst, hi[:, xx, cols], xh[:, :], start=True, stop=False)
                            pe.matmul(dst, hi[:, xx, cols], xl[:, :], start=False, stop=False)
                            pe.matmul(dst, lo[:, xx, cols], xh[:, :], start=False, stop=True).then_inc(full, 1)
                    elif step == "w3":
                        xx, c = divmod(arg, 3)
                        rows = TILES[c]
                        if isinstance(j, int) and j == 1 and arg == 0:
                            pe.wait_ge(w3_in, 96)
                        wait(pe, gated_ready, e, NK, arg + 1)
                        if c == 0:
                            wait(pe, eo_done, e, NX, xx)
                        pe.matmul(eo_bank[:, :], w3_sb[0:rows, xx, c, :], gated[0:rows, arg % ACT_RING, :],
                                  start=(c == 0), stop=(c == 2)).then_inc(w3_done, 1)
                    elif step == "outT":
                        wait(pe, added, e, E, E)
                        side_free(j, parts, step, arg)
                        for i in range(TT):
                            mm = pe.transpose(side[:, i * P:(i + 1) * P], moe[:, i * P:(i + 1) * P], ident[:, :])
                        mm.then_inc(side_full, 1)
                    else:
                        project_in(j, parts, f, step, arg)

            pe.wait_ge(consts, CONSTS)
            pe.wait_ge(small_in, 16 * SMALL)
            for step, arg in FIRST:
                project_in(FRONT, "", (0, 0), step, arg)
            bodies(pe, program)


def kernel(**inputs):
    import numpy as np
    import concourse.bacc as _bacc
    from concourse import mybir as _mybir
    from concourse.bass_utils import run_bass_kernel_spmd as _run

    a = {k: np.asarray(v) for k, v in inputs.items()}
    laid = {
        "x": a["L0_attn_x"], "w_in": a["L0_attn_W_in"], "w_delta": a["L0_attn_W_delta"],
        "b_delta": a["L0_attn_b_delta"].reshape(NH, P).T, "w_b": a["L0_attn_W_B"], "w_c": a["L0_attn_W_C"],
        "a_log": a["L0_attn_A_log"], "d_param": a["L0_attn_D_param"].reshape(NH, P).T, "w_out": a["L0_attn_W_out"],
        "wg_t": a["L0_ffn_Wg"].T, "bias": a["L0_ffn_routing_bias"],
        "w1_t": a["L0_ffn_W1"].transpose(2, 0, 1), "w2_t": a["L0_ffn_W2"].transpose(2, 0, 1),
        "ws1_t": a["L0_ffn_Ws1"].T, "ws2_t": a["L0_ffn_Ws2"].T,
        "w3_t": a["L0_ffn_W3"].transpose(0, 2, 1), "ws3_t": a["L0_ffn_Ws3"].T,
    }
    nc = _bacc.Bacc("TRN2", target_bir_lowering=False, num_devices=1)
    arrays, args = {}, []
    for name, v in laid.items():
        v = np.ascontiguousarray(v)
        arrays[f"{name}_dram"] = v
        args.append(nc.dram_tensor(f"{name}_dram", v.shape, _mybir.dt.from_np(v.dtype), kind="ExternalInput").ap())
    args.append(nc.dram_tensor("out_dram", laid["x"].shape, _mybir.dt.float32, kind="ExternalOutput").ap())
    mamba_moe_kernel(nc, *args)
    r = _run(nc, [arrays], core_ids=[0])
    return r.results[0]["out_dram"]
```

```python
import concourse.bass as bass
from concourse import mybir
from contextlib import ExitStack

F32 = mybir.dt.float32
F32R = mybir.dt.float32r
BF16 = mybir.dt.bfloat16
ALU = mybir.AluOpType
ACT = mybir.ActivationFunctionType
AX = mybir.AxisListType

P = 128
SEQ = 256
TOK = 512
TT = TOK // P
DI = 256
NH = DI // P
NS = 16
GN = 2
NG = NS // GN
NU = NG * NH
E = 8
TOPK = 4
HID = 341
TILES = [128, 128, 85]
NX = E + 1
NK = 3 * NX
EPS = 1e-5

DA_RING = 8
HB_RING = 4
BB_RING = 4
ACT_RING = 9
GATE_STEPS = 13

PE_ORDER = """
d:w3.11 m:turn.2 m:bb.5 d:h12.15 m:turn.3 m:wi_res.1 d:h12.16 m:bb.6 m:turn.4.5 d:wb.2 d:h12.17 m:bb.7
m:turn.6 d:h12.18 m:turn.7.8 d:w3.12 d:wb.3 d:w3.13.14 e:x1T.0 m:turn.9 d:h12.19 e:gate.0 d:h12.20 d:w3.15
m:bb.8 d:w3.16 m:turn.10 d:wb.4 d:h12.21.22 m:turn.11 m:bb.9 d:h12.23 d:w3.17 m:bb.10 d:h12.24 m:turn.12
m:bb.11 m:turn.13 d:h12.25 d:wb.5 d:w3.18 m:turn.14 d:wb.6 m:turn.15 d:h12.26 m:bb.12 d:w3.19 m:turn.16
m:bb.13 d:w3.20 e:h12.0 m:turn.17 d:wb.7 e:h12.1 d:w3.21.22.23 f:xT.0 m:turn.18 d:w3.24 m:turn.19 e:wT.0
m:turn.20 e:h12.2 d:w3.25 f:wi.0 m:turn.21 e:h12.3 f:wi.1 m:turn.22 e:h12.4 m:bb.14 m:turn.23.24 f:bc.0
d:w3.26 m:bb.15 e:h12.5 m:turn.25 f:dz.0 e:h12.6 e:wb.0 m:turn.26 e:h12.7 f:bT.0 m:turn.27.28 f:bb.0 e:h12.8
f:bb.1 e:w3.0 m:turn.29 f:dz.1 e:w3.1.2 d:outT.0 e:h12.9 m:turn.30.31 e:wb.1 e:w3.3 m:turn.32 e:w3.4 f:bb.2
e:w3.5 m:turn.33 e:h12.10 m:yT.0 e:w3.6.7 f:bb.3 e:w3.8 m:yT.1 e:h12.11 e:w3.9 m:wo.0 e:h12.12 f:wi_res.0
e:h12.13.14 f:turn.0 f:bb.4 e:w3.10 f:turn.1
"""
ACT_ORDER = """
m:bb.5 d:silu.15 m:wi_res.1 m:bb.6 d:silu.16 d:wb.2 d:silu.17 m:bb.7 d:silu.18 m:decay.6 d:wb.3 m:decay.7.8
e:x1T.0 m:decay.9 d:silu.19 m:bb.8 d:silu.20.21 d:wb.4 d:silu.22 m:bb.9 d:silu.23 e:gate_exp.0 m:bb.10
d:silu.24 m:bb.11 d:wb.5 d:silu.25 d:wb.6 m:bb.12 d:silu.26 m:bb.13 e:silu.0 m:decay.10 d:wb.7 m:decay.11.12
f:xT.0 m:decay.13 e:silu.1 e:wT.0 e:silu.2 f:wi.0 e:silu.3 f:wi.1 e:silu.4 m:bb.14 m:decay.14 m:bb.15
m:decay.15 e:silu.5.6 e:wb.0 f:bT.0 e:silu.7 f:bb.0 e:silu.8 f:bb.1 f:softplus.0 e:silu.9 e:wb.1 f:decay.0
f:bb.2 f:decay.1.2 f:bb.3 f:decay.3 e:silu.10.11 f:decay.4 e:silu.12.13 f:wi_res.0 e:silu.14 f:decay.5
f:bb.4
"""
DVE_ORDER = """
m:scan.2 d:gated.13.14 m:sum.0 e:x1n.0 m:sum.1 m:scan.3 m:sum.2.3 d:gated.15 m:sum.4 d:gated.16 m:sum.5
d:eo.3 m:sum.6 m:scan.4 d:gated.17 m:sum.7 m:scan.5 m:sum.8 d:gated.18 m:sum.9 d:eo.4 e:gate.0 d:gated.19
m:sum.10 d:gated.20 f:ln.0 d:gated.21.22 m:sum.11 m:scan.6 d:gated.23 d:eo.5 m:scan.7 m:sum.12.13
d:gated.24.25 e:gate_w.0 m:sum.14 e:xsplit.0 d:gated.26 m:sum.15 d:eo.6 m:scan.8 f:xn.0 m:scan.9 m:sum.16.17
d:eo.7 e:gated.0 m:sum.18 m:scan.10 m:sum.19 e:gated.1 m:scan.11 m:sum.20 e:gated.2 m:sum.21.22 m:scan.12
e:gated.3 f:bc.0 m:sum.23.24 m:scan.13 e:gated.4 f:dz.0 e:gated.5 m:sum.25.26 e:gated.6 d:eo.8 m:sum.27
m:scan.14.15 f:dz.1 e:gated.7 m:sum.28.29 d:outT.0 e:eo.0 m:sum.30 f:delta.0 m:sum.31 e:gated.8 m:sum.32.33
e:eo.1 e:gated.9 f:c.0 m:yT.0 f:scan.0 e:eo.2 m:yT.1 f:scan.1 e:gated.10.11 m:wo.0 f:ud.0 e:gated.12
"""
POOL_ORDER = """
m:dbu.2.3 e:rstd1.0 m:xcur.0 m:dbu.4.5 d:add.3 m:dbu.6.7 d:add.4 m:dbu.8.9 f:rstd.0 m:dbu.10 d:add.5
e:wsplit.0 m:dbu.11.12.13 d:add.6 f:bsplit.0 m:dbu.14.15 d:add.7.8 f:du.0 f:dbu.0.1 e:x1k.0 e:add.1.2
"""


def orders():
    steps = {}
    for engine, text in (("pe", PE_ORDER), ("act", ACT_ORDER), ("dve", DVE_ORDER), ("pool", POOL_ORDER)):
        steps[engine] = []
        for entry in text.split():
            part, step = entry.split(":")
            step, *args = step.split(".")
            steps[engine] += [(part, step, int(arg)) for arg in args]
    return steps


def mamba_moe_kernel(nc, x, w_in, w_delta, b_delta, w_b, w_c, a_log, d_param, w_out, wg_t, bias, w1_t, w2_t,
                     ws1_t, ws2_t, w3_t, ws3_t, out):
    NT = x.shape[0] * x.shape[1] // TOK
    steps = orders()
    SIDE = ("xT", "wi", "wi_res", "dz", "bc", "bT", "bb", "yT", "wo", "x1T", "gate", "wT", "wb", "outT")

    SHIFT = {"f": 1, "m": 0, "e": -1, "d": -2}

    def body_parts(j):
        return "".join(part for part, shift in SHIFT.items() if 0 <= j + shift < NT)

    def side_uses(parts):
        return [(p, s, a) for p, s, a in steps["pe"] if s in SIDE and p in parts]

    def side_before(j):
        if isinstance(j, int):
            return sum(len(side_uses(body_parts(i))) for i in range(-1, j))
        per = len(side_uses("fmed"))
        return per * j + (side_before(2) - 2 * per)

    ctx = ExitStack()
    with ctx:
        def sb(name, shape, dt=F32):
            return ctx.enter_context(nc.sbuf_tensor(name, shape, dt))

        def bank(name):
            return ctx.enter_context(nc.psum_tensor(name, [P, 512], F32))

        def sem(name):
            return ctx.enter_context(nc.semaphore(name))

        ident = sb("ident", [P, P])
        ident_bf = sb("ident_bf", [P, P], BF16)
        sel_b = sb("sel_b", [3 * NS, NS, P], BF16)
        sel_w = sb("sel_w", [3 * E, E, P], BF16)
        before = sb("before", [P, E, E])
        half_exp = sb("half_exp", [P, TT])
        w_in_sb = sb("w_in_sb", [P, 2 * DI])
        w_delta_sb = sb("w_delta_sb", [P, NH, DI])
        w_bc_sb = sb("w_bc_sb", [P, NH, 2 * NS])
        w_out_sb = sb("w_out_sb", [P, NH, P])
        a_sb = sb("a_sb", [P, NH, NS])
        a_exp = sb("a_exp", [P, NH, NS])
        bd_sb = sb("bd_sb", [P, NH])
        dp_sb = sb("dp_sb", [P, NH])
        wg_sb = sb("wg_sb", [P, E])
        bias_sb = sb("bias_sb", [P, E])
        w1h = sb("w1h", [P, NX, HID], F32R)
        w1l = sb("w1l", [P, NX, HID], F32R)
        w2h = sb("w2h", [P, NX, HID], F32R)
        w2l = sb("w2l", [P, NX, HID], F32R)
        w3_sb = sb("w3_sb", [P, NX, 3, P])
        x_in = sb("x_in", [P, TT, P])
        x_cur = sb("x_cur", [P, TT, P])
        xn = sb("xn", [P, TT, P])
        xnT = sb("xnT", [P, TOK])
        u = sb("u", [P, NH, TOK])
        sres = sb("sres", [P, NH, TOK])
        delta = sb("delta", [P, NH, TOK])
        y = sb("y", [P, NH, TOK])
        du = sb("du", [P, NH, TOK])
        bc = sb("bc", [P, TT, 2 * NS])
        c_sb = sb("c_sb", [P, TT, NS])
        bparts = sb("bparts", [P, TT, 3, NS], BF16)
        brest = sb("brest", [P, 2, TT, NS])
        bT = sb("bT", [3 * NS, TOK], BF16)
        bbc = sb("bbc", [P, BB_RING, TOK])
        decay = sb("decay", [P, DA_RING, GN, TOK])
        hb = sb("hb", [P, HB_RING, GN, TOK])
        acc = sb("acc", [P, TT, DI])
        one = sb("one", [P, 1])
        stats = {t: sb(f"stats_{t}", [P, TT, 6]) for t in ("x", "x1")}
        mv = {t: sb(f"mv_{t}", [P, TT, 2]) for t in ("x", "x1")}
        veps = {t: sb(f"veps_{t}", [P, TT]) for t in ("x", "x1")}
        rstd = {t: sb(f"rstd_{t}", [P, TT]) for t in ("x", "x1")}
        x1 = sb("x1", [P, TT, P])
        x1k = sb("x1k", [P, TT, P])
        x1n = xn
        x1nT = xnT
        xh = sb("xh", [P, TOK], F32R)
        xl = sb("xl", [P, TOK], F32R)
        g = sb("g", [P, TT, E])
        eo_w = sb("eo_w", [P, 2, TOK])
        cmp_gt, cmp_ge = (y[:, i, 0:TT * E * E].rearrange("p (t e j) -> p t e j", t=TT, e=E) for i in range(2))
        rank = sb("rank", [P, TT, E])
        mask = sb("mask", [P, TT, E])
        gmax = sb("gmax", [P, TT])
        gm = sb("gm", [P, TT, E])
        gex = sb("gex", [P, TT, E])
        gem = sb("gem", [P, TT, E])
        gsum = sb("gsum", [P, TT])
        ginv = sb("ginv", [P, TT])
        w = sb("w", [P, TT, E])
        wparts = sb("wparts", [P, TT, 3, E], BF16)
        wrest = sb("wrest", [P, 2, TT, E])
        wT = sb("wT", [3 * E, TOK], BF16)
        wbc = sb("wbc", [P, 2, TOK])
        s = sb("s", [P, 2, TOK])
        gated = sb("gated", [P, ACT_RING, TOK])
        stage = gated[:, :, :].rearrange("p a t -> p (a t)")[:, 0:NX * HID]
        moe = sb("moe", [P, TOK])

        h1_bank = [bank(f"h1_{i}") for i in range(2)]
        h2_bank = [bank(f"h2_{i}") for i in range(2)]
        eo_bank = bank("eo_bank")
        turn_bank = [bank(f"turn_{i}") for i in range(2)]
        side = bank("side")
        side_bf = side[:, :].bitcast(BF16)

        consts = sem("consts")
        small_in = sem("small_in")
        w1_in, w2_in, w3_in = sem("w1_in"), sem("w2_in"), sem("w3_in")
        a_exped, a_ready = sem("a_exped"), sem("a_ready")
        w_hi, w_lo = sem("w_hi"), sem("w_lo")
        x_in_sem, out_stored = sem("x_in_sem"), sem("out_stored")
        ln_steps = {"x": sem("ln_steps_x"), "x1": sem("ln_steps_x1")}
        rstd_steps = {"x": sem("rstd_steps_x"), "x1": sem("rstd_steps_x1")}
        xn_ready = {"x": sem("xn_ready_x"), "x1": sem("xn_ready_x1")}
        x_cur_ready = sem("x_cur_ready")
        xnT_ready, wi_ready, sres_ready = sem("xnT_ready"), sem("wi_ready"), sem("sres_ready")
        side_full = sem("side_full")
        zb_ready, sp_steps, delta_ready, du_ready = sem("zb_ready"), sem("sp_steps"), sem("delta_ready"), sem("du_ready")
        bc_ready, bparts_steps, bT_ready, bb_ready = sem("bc_ready"), sem("bparts_steps"), sem("bT_ready"), sem("bb_ready")
        dbu_ready, decay_ready, scanned = sem("dbu_ready"), sem("decay_ready"), sem("scanned")
        turned, summed = sem("turned"), sem("summed")
        ud_ready, c_ready, y_ready = sem("ud_ready"), sem("c_ready"), sem("y_ready")
        x1_ready, x1k_ready, x1T_ready, xsplit = sem("x1_ready"), sem("x1k_ready"), sem("x1T_ready"), sem("xsplit")
        gate_steps, gex_ready, wparts_steps, wT_ready, wbc_ready = (
            sem("gate_steps"), sem("gex_ready"), sem("wparts_steps"), sem("wT_ready"), sem("wbc_ready"))
        h1_full, h2_full, s_ready, gated_ready = sem("h1_full"), sem("h2_full"), sem("s_ready"), sem("gated_ready")
        w3_done, eo_done, added, out_ready = sem("w3_done"), sem("eo_done"), sem("added"), sem("out_ready")

        x_t = x.rearrange("b (c p) d -> p (b c) d", p=P)
        out_t = out.rearrange("b (c p) d -> p (b c) d", p=P)

        def wait(eng, s_, turn, per, c):
            j, shift = turn
            value = per * j + (per * shift + c)
            if isinstance(value, int):
                if value <= 0:
                    return
            else:
                assert per * (2 + shift) + c > 0
            eng.wait_ge(s_, value)

        def carry_waits(eng):
            eng.nop(nofuse=True)

        def bodies(eng, program):
            for j in range(-1, 2):
                program(j, body_parts(j))
            with eng.Fori(2, NT - 1) as j:
                program(j, "fmed")
            for j in range(NT - 1, NT + 2):
                program(j, body_parts(j))

        def turn_of(j, part):
            return (j, SHIFT[part])

        def side_index(j, parts, part, step, arg):
            return side_uses(parts).index((part, step, arg)) + 1 + side_before(j)

        def turned_before(grp):
            last = grp - HB_RING // NH
            return 2 + 2 * GN * (last + 1) if last >= 0 else 2 * GN * (last + 1)

        def hidden_ring(k):
            return k - 2 if k >= 2 else (NK - 1 if k == 0 else NK - 2) - NK

        SMALL = 10
        CONSTS = 16
        FILLS = 2 * (NS + 1)
        SUMS = 2 * FILLS
        block = ctx.enter_context(nc.Block())

        @block.sync
        def _(sp_eng):
            def load_x(turn):
                wait(sp_eng, xn_ready["x"], turn, TT, 0)
                carry_waits(sp_eng)
                wait(sp_eng, x_cur_ready, turn, 1, 0)
                at = TT * turn[0] + TT * turn[1]
                carry_waits(sp_eng)
                sp_eng.dma_start(x_in[:, :, :], x_t[:, bass.ds(at, TT), :]).then_inc(x_in_sem, 16)

            def load_weights():
                small = [(w_in_sb[:, :], w_in), (w_delta_sb[:, :, :], w_delta.rearrange("(k p) n -> p k n", p=P)),
                         (w_bc_sb[:, :, 0:NS], w_b.rearrange("(k p) n -> p k n", p=P)),
                         (w_bc_sb[:, :, NS:], w_c.rearrange("(k p) n -> p k n", p=P)),
                         (w_out_sb[:, :, :], w_out.rearrange("(k p) n -> p k n", p=P)),
                         (a_sb[:, :, :], a_log.rearrange("(k p) n -> p k n", p=P)),
                         (bd_sb[:, :], b_delta),
                         (dp_sb[:, :], d_param),
                         (wg_sb[:, :], wg_t), (bias_sb[:, :], bias.partition_broadcast(P))]
                for dst, src in small:
                    sp_eng.dma_start(dst, src).then_inc(small_in, 16)
                assert len(small) == SMALL
                sp_eng.dma_start(stage[:, 0:HID], ws1_t).then_inc(w1_in, 16)
                sp_eng.dma_start(stage[:, HID:].rearrange("p (e h) -> p e h", e=E), w1_t).then_inc(w1_in, 16)
                for c, rows in enumerate(TILES):
                    sp_eng.dma_start(w3_sb[0:rows, 0, c, :], ws3_t[P * c:P * c + rows, :]).then_inc(w3_in, 16)
                    sp_eng.dma_start(w3_sb[0:rows, 1:, c, :],
                                     w3_t[:, P * c:P * c + rows, :].rearrange("e h d -> h e d")).then_inc(w3_in, 16)

            def load_w2():
                sp_eng.wait_ge(w_lo, 1)
                sp_eng.dma_start(stage[:, 0:HID], ws2_t).then_inc(w2_in, 16)
                sp_eng.dma_start(stage[:, HID:].rearrange("p (e h) -> p e h", e=E), w2_t).then_inc(w2_in, 16)

            def program(j, parts):
                if "f" in parts:
                    load_x(turn_of(j, "f"))
                if isinstance(j, int) and j == -1:
                    load_weights()
                if isinstance(j, int) and j == 0:
                    load_w2()
                if "d" in parts:
                    wait(sp_eng, out_ready, turn_of(j, "d"), 1, 1)
                    at = TT * j + TT * SHIFT["d"]
                    carry_waits(sp_eng)
                    sp_eng.dma_start(out_t[:, bass.ds(at, TT), :], x1k[:, :, :]).then_inc(out_stored, 16)

            bodies(sp_eng, program)
            sp_eng.wait_ge(out_stored, 16 * NT)

        @block.gpsimd
        def _(pool):
            pool.memset(ident[:, :], 0.0).then_inc(consts, 1)
            pool.memset(sel_b[:, :, :], 0.0).then_inc(consts, 1)
            pool.memset(sel_w[:, :, :], 0.0).then_inc(consts, 1)
            pool.memset(before[:, :, :], 1.0).then_inc(consts, 1)
            pool.wait_ge(consts, 4)
            pool.affine_select(out=ident[:, :], in_=ident[:, :], compare_op=ALU.not_equal, fill=1.0, base=0,
                               pattern=[[-1, P]], channel_multiplier=1).then_inc(consts, 1)
            pool.affine_select(out=before[:, :, :], in_=before[:, :, :], compare_op=ALU.is_ge, fill=0.0, base=-1,
                               pattern=[[1, E], [-1, E]], channel_multiplier=0).then_inc(consts, 1)
            for i in range(3):
                pool.wait_ge(consts, 6 + 2 * i)
                pool.affine_select(out=sel_b[:, :, :], in_=sel_b[:, :, :], compare_op=ALU.not_equal, fill=1.0,
                                   base=-NS * i, pattern=[[-1, NS], [0, P]], channel_multiplier=1).then_inc(consts, 1)
                pool.affine_select(out=sel_w[:, :, :], in_=sel_w[:, :, :], compare_op=ALU.not_equal, fill=1.0,
                                   base=-E * i, pattern=[[-1, E], [0, P]], channel_multiplier=1).then_inc(consts, 1)
            pool.tensor_copy(ident_bf[:, :], ident[:, :]).then_inc(consts, 1)
            pool.memset(half_exp[:, :], -0.5).then_inc(consts, 1)
            pool.memset(one[:, :], 1.0).then_inc(consts, 1)
            pool.memset(decay[:, :, :, :].rearrange("p r n (b t) -> p (r n b) t", t=SEQ)[:, :, 0:1], 0.0).then_inc(consts, 1)

            def take_rstd(norm, turn):
                wait(pool, ln_steps[norm], turn, 2 * TT, 2 * TT)
                wait(pool, xn_ready[norm], turn, TT, 0)
                carry_waits(pool)
                pool.tensor_scalar(veps[norm][:, :], mv[norm][:, :, 1], EPS, 1.0, ALU.add, ALU.mult)\
                    .then_inc(rstd_steps[norm], 1)
                wait(pool, rstd_steps[norm], turn, 2, 1)
                pool.tensor_tensor(rstd[norm][:, :], veps[norm][:, :], half_exp[:, :], ALU.pow)\
                    .then_inc(rstd_steps[norm], 1)

            def cut(parts_tile, rest, src, steps_sem, turn):
                for i in range(3):
                    cur = src if i == 0 else rest[:, i - 1]
                    if i:
                        wait(pool, steps_sem, turn, 5, 2 * i)
                    carry_waits(pool)
                    pool.tensor_copy(parts_tile[:, :, i, :], cur).then_inc(steps_sem, 1)
                    if i < 2:
                        wait(pool, steps_sem, turn, 5, 2 * i + 1)
                        pool.tensor_tensor(rest[:, i], cur, parts_tile[:, :, i, :], ALU.subtract)\
                            .then_inc(steps_sem, 1)

            def program(j, parts):
                for part, step, arg in steps["pool"]:
                    if part not in parts:
                        continue
                    turn = turn_of(j, part)
                    if step == "bsplit":
                        wait(pool, bc_ready, turn, 1, 1)
                        wait(pool, bT_ready, turn, 1, 0)
                        cut(bparts, brest, bc[:, :, 0:NS], bparts_steps, turn)
                    elif step == "du":
                        wait(pool, delta_ready, turn, 1, 1)
                        wait(pool, dbu_ready, turn, NU, 0)
                        pool.tensor_tensor(du[:, :, :], delta[:, :, :], u[:, :, :], ALU.mult).then_inc(du_ready, 1)
                    elif step == "dbu":
                        grp, h = divmod(arg, NH)
                        wait(pool, du_ready, turn, 1, 1)
                        wait(pool, bb_ready, turn, NS, GN * grp + GN)
                        wait(pool, turned, turn, FILLS, turned_before(grp))
                        r = GN * grp % BB_RING
                        pool.tensor_tensor(hb[:, arg % HB_RING, :, :],
                                           du[:, h, :].unsqueeze(1).broadcast_to((P, GN, TOK)),
                                           bbc[:, r:r + GN, :], ALU.mult).then_inc(dbu_ready, 1)
                    elif step == "rstd1":
                        take_rstd("x1", turn)
                    elif step == "rstd":
                        take_rstd("x", turn)
                    elif step == "wsplit":
                        wait(pool, gate_steps, turn, GATE_STEPS, GATE_STEPS)
                        wait(pool, wT_ready, turn, 1, 0)
                        cut(wparts, wrest, w[:, :, :], wparts_steps, turn)
                    elif step == "x1k":
                        wait(pool, x1_ready, turn, 1, 1)
                        wait(pool, out_stored, turn, 16, 0)
                        carry_waits(pool)
                        pool.tensor_copy(x1k[:, :, :], x1[:, :, :]).then_inc(x1k_ready, 1)
                    elif step == "xcur":
                        wait(pool, x_in_sem, turn, 16, 16)
                        wait(pool, x1_ready, turn, 1, 0)
                        carry_waits(pool)
                        pool.tensor_copy(x_cur[:, :, :], x_in[:, :, :]).then_inc(x_cur_ready, 1)
                    elif step == "add":
                        wait(pool, eo_done, turn, NX, arg + 1)
                        wait(pool, added, turn, E, arg - 1)
                        pool.tensor_tensor(moe[:, :], moe[:, :], eo_w[:, arg % 2, :], ALU.add).then_inc(added, 1)

            bodies(pool, program)

        @block.scalar
        def _(act):
            def read_side(j, parts, part, step, arg, out_ap, in_ap, func, ready):
                act.wait_ge(side_full, side_index(j, parts, part, step, arg))
                act.activation(out_ap, in_ap, func).then_inc(ready, 1)

            def program(j, parts):
                for part, step, arg in steps["act"]:
                    if part not in parts:
                        continue
                    turn = turn_of(j, part)
                    if step == "x1T":
                        read_side(j, parts, part, step, arg, x1nT[:, :], side[:, :], ACT.Copy, x1T_ready)
                    elif step == "softplus":
                        act.preload_act_table_set("natural_log_exp_and_others")
                        wait(act, zb_ready, turn, NH, NH)
                        wait(act, dbu_ready, turn, NU, 0)
                        act.activation(du[:, :, :], delta[:, :, :], ACT.Abs).then_inc(sp_steps, 1)
                        wait(act, sp_steps, turn, 3, 1)
                        act.activation(du[:, :, :], du[:, :, :], ACT.Exp, scale=-1.0).then_inc(sp_steps, 1)
                        wait(act, sp_steps, turn, 3, 2)
                        act.activation(du[:, :, :], du[:, :, :], ACT.Ln, bias=one[:, :]).then_inc(sp_steps, 1)
                    elif step == "bT":
                        read_side(j, parts, part, step, arg, bT[:, :], side_bf[0:3 * NS, 0:TOK], ACT.Copy, bT_ready)
                    elif step == "bb":
                        wait(act, dbu_ready, turn, NU, NH * ((arg - BB_RING) // GN + 1))
                        read_side(j, parts, part, step, arg, bbc[:, arg % BB_RING, :], side[:, :], ACT.Copy, bb_ready)
                    elif step == "decay":
                        grp, h = divmod(arg, NH)
                        wait(act, delta_ready, turn, 1, 1)
                        wait(act, scanned, turn, NU, arg - DA_RING + 1)
                        for i in range(GN):
                            act.activation(
                                decay[:, arg % DA_RING, i, :].rearrange("p (b t) -> p b t", t=SEQ)[:, :, 1:],
                                delta[:, h, :].rearrange("p (b t) -> p b t", t=SEQ)[:, :, 1:],
                                ACT.Exp, scale=a_sb[:, h, GN * grp + i:GN * grp + i + 1]).then_inc(decay_ready, 1)
                    elif step == "gate_exp":
                        wait(act, gate_steps, turn, GATE_STEPS, 9)
                        act.activation(gex[:, :, :], gm[:, :, :], ACT.Exp).then_inc(gex_ready, 1)
                    elif step == "wT":
                        read_side(j, parts, part, step, arg, wT[:, :], side_bf[0:3 * E, 0:TOK], ACT.Copy, wT_ready)
                    elif step == "wb":
                        wait(act, eo_done, turn, NX, arg if arg >= 2 else arg - 1)
                        read_side(j, parts, part, step, arg, wbc[:, arg % 2, :], side[:, :], ACT.Copy, wbc_ready)
                    elif step == "silu":
                        rows = TILES[arg % 3]
                        wait(act, h1_full, turn, NK, arg + 1)
                        wait(act, gated_ready, turn, NK, hidden_ring(arg) + 1)
                        act.activation(s[0:rows, arg % 2, :], h1_bank[arg % 2][0:rows, :], ACT.Silu)\
                           .then_inc(s_ready, 1)
                    elif step == "xT":
                        wait(act, xsplit, turn, 2, -2)
                        wait(act, gate_steps, turn, GATE_STEPS, -GATE_STEPS)
                        read_side(j, parts, part, step, arg, xnT[:, :], side[:, :], ACT.Copy, xnT_ready)
                    elif step == "wi":
                        wait(act, du_ready, turn, 1, 0)
                        wait(act, turned, turn, FILLS, 2 - FILLS)
                        read_side(j, parts, part, step, arg, u[:, arg, :], side[:, :], ACT.Silu, wi_ready)
                    elif step == "wi_res":
                        wait(act, y_ready, turn, NH, 0)
                        read_side(j, parts, part, step, arg, sres[:, arg, :], side[:, :], ACT.Silu, sres_ready)
                    if isinstance(j, int) and j + SHIFT[part] == 0 and step == "decay" and arg in (4, 10):
                        cut_hi(arg == 10)

            def cut_hi(second):
                act.wait_ge(w2_in if second else w1_in, 32)
                dst = w2h if second else w1h
                act.activation(dst[:, :, :].rearrange("p x h -> p (x h)"), stage, ACT.Copy).then_inc(w_hi, 1)

            act.wait_ge(small_in, 16 * SMALL)
            act.activation(a_exp[:, :, :], a_sb[:, :, :], ACT.Exp).then_inc(a_exped, 1)
            act.wait_ge(consts, CONSTS)
            act.wait_ge(a_ready, 1)
            bodies(act, program)

        @block.vector
        def _(dve):
            def take_stats(norm, src, turn):
                for i in range(TT):
                    dve.bn_stats(stats[norm][:, i, :], src[:, i, :]).then_inc(ln_steps[norm], 1)
                for i in range(TT):
                    wait(dve, ln_steps[norm], turn, 2 * TT, i + 1)
                    carry_waits(dve)
                    dve.bn_aggr(mv[norm][:, i, :], stats[norm][:, i, :]).then_inc(ln_steps[norm], 1)

            def normalize(norm, src, dst, turn):
                wait(dve, rstd_steps[norm], turn, 2, 2)
                for i in range(TT):
                    dve.tensor_scalar(dst[:, i, :], src[:, i, :], mv[norm][:, i, 0:1], rstd[norm][:, i:i + 1],
                                      ALU.subtract, ALU.mult).then_inc(xn_ready[norm], 1)

            def side_wait(j, parts, part, step, arg):
                dve.wait_ge(side_full, side_index(j, parts, part, step, arg))

            def cut_lo(second):
                dve.wait_ge(w_hi, 2 if second else 1)
                hi, lo = (w2h, w2l) if second else (w1h, w1l)
                dve.tensor_tensor(lo[:, :, :].rearrange("p x h -> p (x h)"), stage,
                                  hi[:, :, :].rearrange("p x h -> p (x h)").bitcast(F32), ALU.subtract).then_inc(w_lo, 1)

            def program(j, parts):
                for part, step, arg in steps["dve"]:
                    if part not in parts:
                        continue
                    turn = turn_of(j, part)
                    if step == "dz":
                        wait(dve, decay_ready, turn, NS * NH, 0)
                        wait(dve, du_ready, turn, 1, 0)
                        side_wait(j, parts, part, "dz", arg)
                        dve.tensor_scalar(delta[:, arg, :], side[:, :], bd_sb[:, arg:arg + 1], None, ALU.add)\
                           .then_inc(zb_ready, 1)
                    elif step == "bc":
                        wait(dve, bparts_steps, turn, 5, 0)
                        wait(dve, c_ready, turn, 1, 0)
                        side_wait(j, parts, part, "bc", 0)
                        dve.tensor_copy(bc[:, :, :], side[:, 0:TT * 2 * NS].rearrange("p (t n) -> p t n", t=TT))\
                           .then_inc(bc_ready, 1)
                    elif step == "delta":
                        wait(dve, sp_steps, turn, 3, 3)
                        dve.scalar_tensor_tensor(delta[:, :, :], delta[:, :, :], 0.0, du[:, :, :], ALU.max, ALU.add)\
                           .then_inc(delta_ready, 1)
                    elif step == "scan":
                        wait(dve, decay_ready, turn, NS * NH, GN * (arg + 1))
                        wait(dve, dbu_ready, turn, NU, arg + 1)
                        states = hb[:, arg % HB_RING, :, :].rearrange("p n t -> p (n t)")
                        dve.tensor_tensor_scan(states,
                                               decay[:, arg % DA_RING, :, :].rearrange("p n t -> p (n t)"),
                                               states, 0.0, ALU.mult, ALU.add).then_inc(scanned, 1)
                    elif step == "c":
                        wait(dve, bc_ready, turn, 1, 1)
                        wait(dve, summed, turn, SUMS, 0)
                        dve.tensor_copy(c_sb[:, :, :], bc[:, :, NS:]).then_inc(c_ready, 1)
                    elif step == "ud":
                        wait(dve, wi_ready, turn, NH, NH)
                        for h in range(NH):
                            dve.tensor_scalar(y[:, h, :], u[:, h, :], dp_sb[:, h:h + 1], None, ALU.mult)\
                               .then_inc(ud_ready, 1)
                    elif step == "sum":
                        n, pair = arg // 2 - 1, arg % 2
                        wait(dve, turned, turn, FILLS, arg + 1)
                        if n == 0:
                            wait(dve, c_ready, turn, 1, 1)
                        if n >= 0:
                            wait(dve, summed, turn, SUMS, 2 * arg - 2)
                        for i in range(2):
                            blk = 2 * pair + i
                            hT = turn_bank[pair][:, i * DI:(i + 1) * DI]
                            if n >= 0:
                                ins = dve.scalar_tensor_tensor(acc[:, blk, :], hT, c_sb[:, blk, n:n + 1], acc[:, blk, :],
                                                               ALU.mult, ALU.add)
                            else:
                                ins = dve.tensor_copy(acc[:, blk, :], hT)
                            ins.then_inc(summed, 1)
                    elif step == "yT":
                        wait(dve, sres_ready, turn, NH, NH)
                        side_wait(j, parts, part, "yT", arg)
                        dve.tensor_tensor(y[:, arg, :], side[:, :], sres[:, arg, :], ALU.mult).then_inc(y_ready, 1)
                    elif step == "wo":
                        wait(dve, x_cur_ready, turn, 1, 1)
                        wait(dve, x1k_ready, turn, 1, 0)
                        wait(dve, xn_ready["x1"], turn, TT, 0)
                        side_wait(j, parts, part, "wo", 0)
                        dve.tensor_tensor(x1[:, :, :], side[:, :].rearrange("p (t d) -> p t d", t=TT), x_cur[:, :, :],
                                          ALU.add).then_inc(x1_ready, 1)
                        wait(dve, x1_ready, turn, 1, 1)
                        take_stats("x1", x1, turn)
                    elif step == "x1n":
                        if not (isinstance(j, int) and j + SHIFT[part] == NT - 1):
                            wait(dve, xnT_ready, turn, 1, 2)
                        normalize("x1", x1, x1n, turn)
                    elif step == "gate":
                        def then(c, ins):
                            ins.then_inc(gate_steps, 1)
                            wait(dve, gate_steps, turn, GATE_STEPS, c)

                        side_wait(j, parts, part, "gate", 0)
                        then(1, dve.tensor_tensor(g[:, :, :], side[:, 0:TT * E].rearrange("p (t e) -> p t e", t=TT),
                                                  bias_sb[:, :].unsqueeze(1).broadcast_to((P, TT, E)), ALU.add))
                        gj = g[:, :, :].unsqueeze(2).broadcast_to((P, TT, E, E))
                        ge = g[:, :, :].unsqueeze(3).broadcast_to((P, TT, E, E))
                        then(2, dve.tensor_tensor(cmp_gt[:, :, :, :], gj, ge, ALU.is_gt))
                        then(3, dve.tensor_tensor(cmp_ge[:, :, :, :], gj, ge, ALU.is_ge))
                        then(4, dve.tensor_tensor(cmp_ge[:, :, :, :], cmp_ge[:, :, :, :],
                                                  before[:, :, :].unsqueeze(1).broadcast_to((P, TT, E, E)), ALU.mult))
                        then(5, dve.tensor_tensor(cmp_gt[:, :, :, :], cmp_gt[:, :, :, :], cmp_ge[:, :, :, :], ALU.max))
                        then(6, dve.tensor_reduce(rank[:, :, :], cmp_gt[:, :, :, :], AX.X, ALU.add))
                        then(7, dve.tensor_scalar(mask[:, :, :], rank[:, :, :], TOPK - 0.5, None, ALU.is_lt))
                        then(8, dve.tensor_reduce(gmax[:, :], g[:, :, :], AX.X, ALU.max))
                        then(9, dve.tensor_tensor(gm[:, :, :], g[:, :, :],
                                                  gmax[:, :].unsqueeze(2).broadcast_to((P, TT, E)), ALU.subtract))
                    elif step == "gate_w":
                        def then(c, ins):
                            ins.then_inc(gate_steps, 1)
                            wait(dve, gate_steps, turn, GATE_STEPS, c)

                        wait(dve, gex_ready, turn, 1, 1)
                        wait(dve, wparts_steps, turn, 5, 0)
                        then(10, dve.tensor_tensor(gem[:, :, :], gex[:, :, :], mask[:, :, :], ALU.mult))
                        then(11, dve.tensor_reduce(gsum[:, :], gem[:, :, :], AX.X, ALU.add))
                        then(12, dve.reciprocal(ginv[:, :], gsum[:, :]))
                        then(13, dve.tensor_tensor(w[:, :, :], gem[:, :, :],
                                                   ginv[:, :].unsqueeze(2).broadcast_to((P, TT, E)), ALU.mult))
                    elif step == "gated":
                        rows = TILES[arg % 3]
                        wait(dve, h2_full, turn, NK, arg + 1)
                        wait(dve, s_ready, turn, NK, arg + 1)
                        wait(dve, w3_done, turn, NK, arg - ACT_RING + 1)
                        dve.tensor_tensor(gated[0:rows, arg % ACT_RING, :], h2_bank[arg % 2][0:rows, :],
                                          s[0:rows, arg % 2, :], ALU.mult).then_inc(gated_ready, 1)
                    elif step == "eo":
                        wait(dve, w3_done, turn, NK, 3 * arg + 3)
                        if arg == 0:
                            dve.tensor_copy(moe[:, :], eo_bank[:, :]).then_inc(eo_done, 1)
                        else:
                            wait(dve, wbc_ready, turn, E, arg)
                            wait(dve, added, turn, E, arg - 2)
                            dve.tensor_tensor(eo_w[:, arg % 2, :], eo_bank[:, :], wbc[:, (arg - 1) % 2, :], ALU.mult)\
                               .then_inc(eo_done, 1)
                    elif step == "outT":
                        wait(dve, x1k_ready, turn, 1, 1)
                        side_wait(j, parts, part, "outT", 0)
                        dve.tensor_tensor(x1k[:, :, :], side[:, :].rearrange("p (t d) -> p t d", t=TT), x1k[:, :, :],
                                          ALU.add).then_inc(out_ready, 1)
                    elif step == "xsplit":
                        wait(dve, x1T_ready, turn, 1, 1)
                        wait(dve, h2_full, turn, NK, 0)
                        dve.tensor_copy(xh[:, :], x1nT[:, :]).then_inc(xsplit, 1)
                        wait(dve, xsplit, turn, 2, 1)
                        dve.tensor_tensor(xl[:, :], x1nT[:, :], xh[:, :].bitcast(F32), ALU.subtract).then_inc(xsplit, 1)
                    elif step == "ln":
                        wait(dve, x_in_sem, turn, 16, 16)
                        take_stats("x", x_in, turn)
                    elif step == "xn":
                        wait(dve, x1T_ready, turn, 1, -1)
                        normalize("x", x_in, xn, turn)
                    if isinstance(j, int) and j + SHIFT[part] == 0 and step == "scan" and arg in (4, 10):
                        cut_lo(arg == 10)

            dve.wait_ge(a_exped, 1)
            dve.tensor_scalar(a_sb[:, :, :], a_exp[:, :, :], -1.0, None, ALU.mult).then_inc(a_ready, 1)
            dve.wait_ge(consts, CONSTS)
            bodies(dve, program)

        @block.tensor
        def _(pe):
            SIDE_READ = {"xT": (xnT_ready, 1), "wi": (wi_ready, NH), "wi_res": (sres_ready, NH), "dz": (zb_ready, NH),
                         "bc": (bc_ready, 1), "bT": (bT_ready, 1), "bb": (bb_ready, NS), "yT": (y_ready, NH),
                         "wo": (x1_ready, 1), "x1T": (x1T_ready, 1), "gate": (gate_steps, GATE_STEPS),
                         "wT": (wT_ready, 1), "wb": (wbc_ready, E), "outT": (out_ready, 1)}

            def side_free(j, parts, part, step, arg):
                uses = side_uses(parts)
                n = uses.index((part, step, arg))
                if n:
                    last_part, last_step, last_arg = uses[n - 1]
                    turn = turn_of(j, last_part)
                elif isinstance(j, int) and j == -1:
                    return
                else:
                    uses = side_uses(body_parts(j - 1) if isinstance(j, int) else "fmed")
                    last_part, last_step, last_arg = uses[-1]
                    turn = (j, SHIFT[last_part] - 1)
                reader, per = SIDE_READ[last_step]
                wait(pe, reader, turn, per, last_arg + 1)

            def program(j, parts):
                for part, step, arg in steps["pe"]:
                    if part not in parts:
                        continue
                    turn = turn_of(j, part)
                    if step == "x1T":
                        wait(pe, xn_ready["x1"], turn, TT, TT)
                        side_free(j, parts, part, step, arg)
                        for i in range(TT):
                            mm = pe.transpose(side[:, i * P:(i + 1) * P], x1n[:, i, :], ident[:, :])
                        mm.then_inc(side_full, 1)
                    elif step == "dz":
                        wait(pe, wi_ready, turn, NH, NH)
                        side_free(j, parts, part, step, arg)
                        for k in range(NH):
                            mm = pe.matmul(side[:, :], w_delta_sb[:, k, arg * P:(arg + 1) * P], u[:, k, :],
                                           start=(k == 0), stop=(k == NH - 1))
                        mm.then_inc(side_full, 1)
                    elif step == "bc":
                        wait(pe, wi_ready, turn, NH, NH)
                        side_free(j, parts, part, step, arg)
                        for i in range(TT):
                            for k in range(NH):
                                mm = pe.matmul(side[:, i * 2 * NS:(i + 1) * 2 * NS], u[:, k, i * P:(i + 1) * P],
                                               w_bc_sb[:, k, :], start=(k == 0), stop=(k == NH - 1))
                        mm.then_inc(side_full, 1)
                    elif step == "gate":
                        wait(pe, x1T_ready, turn, 1, 1)
                        side_free(j, parts, part, step, arg)
                        for i in range(TT):
                            mm = pe.matmul(side[:, i * E:(i + 1) * E], x1nT[:, i * P:(i + 1) * P], wg_sb[:, :],
                                           start=True, stop=True)
                        mm.then_inc(side_full, 1)
                    elif step == "bT":
                        wait(pe, bparts_steps, turn, 5, 5)
                        side_free(j, parts, part, step, arg)
                        carry_waits(pe)
                        for i in range(TT):
                            mm = pe.transpose(side_bf[0:3 * NS, i * P:(i + 1) * P],
                                              bparts[:, i, :, :].rearrange("p c n -> p (c n)"), ident_bf[:, :])
                        mm.then_inc(side_full, 1)
                    elif step == "bb":
                        wait(pe, bT_ready, turn, 1, 1)
                        side_free(j, parts, part, step, arg)
                        pe.matmul(side[:, :], sel_b[:, arg, :], bT[:, :], start=True, stop=True).then_inc(side_full, 1)
                    elif step == "wT":
                        wait(pe, wparts_steps, turn, 5, 5)
                        side_free(j, parts, part, step, arg)
                        carry_waits(pe)
                        for i in range(TT):
                            mm = pe.transpose(side_bf[0:3 * E, i * P:(i + 1) * P],
                                              wparts[:, i, :, :].rearrange("p c n -> p (c n)"), ident_bf[:, :])
                        mm.then_inc(side_full, 1)
                    elif step == "wb":
                        wait(pe, wT_ready, turn, 1, 1)
                        side_free(j, parts, part, step, arg)
                        pe.matmul(side[:, :], sel_w[:, arg, :], wT[:, :], start=True, stop=True).then_inc(side_full, 1)
                    elif step == "turn":
                        n, pair = arg // 2 - 1, arg % 2
                        grp, i_n = divmod(n, GN)
                        if n < 0:
                            wait(pe, ud_ready, turn, NH, NH)
                        else:
                            wait(pe, scanned, turn, NU, NH * (grp + 1))
                        wait(pe, summed, turn, SUMS, 2 * arg - 2)
                        for i in range(2):
                            blk = 2 * pair + i
                            for h in range(NH):
                                src = y[:, h, :] if n < 0 else hb[:, (NH * grp + h) % HB_RING, i_n, :]
                                mm = pe.transpose(turn_bank[pair][:, (NH * i + h) * P:(NH * i + h + 1) * P],
                                                  src[:, blk * P:(blk + 1) * P], ident[:, :])
                        mm.then_inc(turned, 1)
                    elif step == "yT":
                        wait(pe, summed, turn, SUMS, SUMS)
                        side_free(j, parts, part, step, arg)
                        for i in range(TT):
                            mm = pe.transpose(side[:, i * P:(i + 1) * P], acc[:, i, arg * P:(arg + 1) * P], ident[:, :])
                        mm.then_inc(side_full, 1)
                    elif step == "wo":
                        wait(pe, y_ready, turn, NH, NH)
                        side_free(j, parts, part, step, arg)
                        for i in range(TT):
                            for k in range(NH):
                                mm = pe.matmul(side[:, i * P:(i + 1) * P], y[:, k, i * P:(i + 1) * P], w_out_sb[:, k, :],
                                               start=(k == 0), stop=(k == NH - 1))
                        mm.then_inc(side_full, 1)
                    elif step == "h12":
                        xx, c = divmod(arg, 3)
                        rows = TILES[c]
                        cols = slice(c * P, c * P + rows)
                        if arg == 0:
                            wait(pe, xsplit, turn, 2, 2)
                            if isinstance(j, int) and j == 1:
                                pe.wait_ge(w_lo, 2)
                        for banks, hi, lo, free, full in ((h1_bank, w1h, w1l, s_ready, h1_full),
                                                          (h2_bank, w2h, w2l, gated_ready, h2_full)):
                            wait(pe, free, turn, NK, hidden_ring(arg) + 1)
                            dst = banks[arg % 2][0:rows, :]
                            pe.matmul(dst, hi[:, xx, cols], xh[:, :], start=True, stop=False)
                            pe.matmul(dst, hi[:, xx, cols], xl[:, :], start=False, stop=False)
                            pe.matmul(dst, lo[:, xx, cols], xh[:, :], start=False, stop=True).then_inc(full, 1)
                    elif step == "w3":
                        xx, c = divmod(arg, 3)
                        rows = TILES[c]
                        if isinstance(j, int) and j == 1 and arg == 0:
                            pe.wait_ge(w3_in, 96)
                        wait(pe, gated_ready, turn, NK, arg + 1)
                        if c == 0:
                            wait(pe, eo_done, turn, NX, xx)
                        pe.matmul(eo_bank[:, :], w3_sb[0:rows, xx, c, :], gated[0:rows, arg % ACT_RING, :],
                                  start=(c == 0), stop=(c == 2)).then_inc(w3_done, 1)
                    elif step == "outT":
                        wait(pe, added, turn, E, E)
                        side_free(j, parts, part, step, arg)
                        for i in range(TT):
                            mm = pe.transpose(side[:, i * P:(i + 1) * P], moe[:, i * P:(i + 1) * P], ident[:, :])
                        mm.then_inc(side_full, 1)
                    elif step == "xT":
                        wait(pe, xn_ready["x"], turn, TT, TT)
                        side_free(j, parts, part, step, arg)
                        for i in range(TT):
                            mm = pe.transpose(side[:, i * P:(i + 1) * P], xn[:, i, :], ident[:, :])
                        mm.then_inc(side_full, 1)
                    elif step in ("wi", "wi_res"):
                        wait(pe, xnT_ready, turn, 1, 1)
                        side_free(j, parts, part, step, arg)
                        tile = arg + (NH if step == "wi_res" else 0)
                        pe.matmul(side[:, :], w_in_sb[:, tile * P:(tile + 1) * P], xnT[:, :], start=True, stop=True)\
                          .then_inc(side_full, 1)

            pe.wait_ge(consts, CONSTS)
            pe.wait_ge(small_in, 16 * SMALL)
            bodies(pe, program)


def kernel(**inputs):
    import numpy as np
    import concourse.bacc as _bacc
    from concourse import mybir as _mybir
    from concourse.bass_utils import run_bass_kernel_spmd as _run

    a = {k: np.asarray(v) for k, v in inputs.items()}
    laid = {
        "x": a["L0_attn_x"], "w_in": a["L0_attn_W_in"], "w_delta": a["L0_attn_W_delta"],
        "b_delta": a["L0_attn_b_delta"].reshape(NH, P).T, "w_b": a["L0_attn_W_B"], "w_c": a["L0_attn_W_C"],
        "a_log": a["L0_attn_A_log"], "d_param": a["L0_attn_D_param"].reshape(NH, P).T, "w_out": a["L0_attn_W_out"],
        "wg_t": a["L0_ffn_Wg"].T, "bias": a["L0_ffn_routing_bias"],
        "w1_t": a["L0_ffn_W1"].transpose(2, 0, 1), "w2_t": a["L0_ffn_W2"].transpose(2, 0, 1),
        "ws1_t": a["L0_ffn_Ws1"].T, "ws2_t": a["L0_ffn_Ws2"].T,
        "w3_t": a["L0_ffn_W3"].transpose(0, 2, 1), "ws3_t": a["L0_ffn_Ws3"].T,
    }
    nc = _bacc.Bacc("TRN2", target_bir_lowering=False, num_devices=1)
    arrays, args = {}, []
    for name, v in laid.items():
        v = np.ascontiguousarray(v)
        arrays[f"{name}_dram"] = v
        args.append(nc.dram_tensor(f"{name}_dram", v.shape, _mybir.dt.from_np(v.dtype), kind="ExternalInput").ap())
    args.append(nc.dram_tensor("out_dram", laid["x"].shape, _mybir.dt.float32, kind="ExternalOutput").ap())
    mamba_moe_kernel(nc, *args)
    r = _run(nc, [arrays], core_ids=[0])
    return r.results[0]["out_dram"]
```

```python
import concourse.bass as bass
from concourse import mybir
from contextlib import ExitStack

F32 = mybir.dt.float32
F32R = mybir.dt.float32r
BF16 = mybir.dt.bfloat16
U16 = mybir.dt.uint16
ALU = mybir.AluOpType
ACT = mybir.ActivationFunctionType
AX = mybir.AxisListType

P = 128
SEQ = 256
TOK = 512
TT = TOK // P
DI = 256
NH = DI // P
NS = 16
GN = 2
NG = NS // GN
NU = NG * NH
E = 8
TOPK = 4
HID = 341
HIDDEN = (E + 1) * HID
NK = -(-HIDDEN // P)
K_ONE = HID // P
NW = NK - K_ONE
EPS = 1e-5

DA_RING = 8
HB_RING = 4
BB_RING = 4
ACT_RING = 8
S_RING = 3
GATE_STEPS = 13

PE_ORDER = """
d:h12.9 e:yT.0 d:w3.3 d:wb.6 d:h12.10 e:yT.1 d:h12.11 e:wo.0 d:w3.4 m:bb.4 d:w3.5.6 m:bb.5 m:turn.0.1 d:wb.7
d:h12.12 m:turn.2 d:wb.8 m:turn.3 d:h12.13 m:wi_res.0 m:turn.4.5 d:wb.9 d:h12.14 m:bb.6 d:w3.7 d:wb.10
d:h12.15 d:wb.11 m:turn.6.7 m:wi_res.1 d:h12.16 d:wb.12 d:h12.17 m:bb.7 d:w3.8 m:turn.8 m:bb.8 d:w3.9
m:turn.9.10 e:x1T.0 d:w3.10 d:wb.13 m:turn.11 d:w3.11 m:turn.12 e:gate.0 d:w3.12 m:bb.9 d:w3.13 m:turn.13
d:wb.14 d:h12.18 m:bb.10 d:w3.14.15 m:bb.11 d:h12.19 m:turn.14 d:wb.15 d:h12.20 m:bb.12 d:h12.21 d:wb.16
d:h12.22 d:wb.17 d:h12.23 m:turn.15 f:xT.0 d:w3.16 m:turn.16.17 d:wb.18 d:w3.17.18 f:wi.0 m:turn.18.19
m:bb.13 e:h12.0 m:bb.14 m:turn.20.21 d:wb.19 d:w3.19 m:bb.15 d:w3.20 d:wb.20 e:h12.1 f:wi.1 d:w3.21 d:wb.21
e:h12.2 f:bc.0 m:turn.22 f:dz.0 d:w3.22 e:wT.0 m:turn.23.24 f:bT.0 m:turn.25 e:wb.0 e:h12.3 f:bb.0 d:w3.23
e:wb.1 e:h12.4 e:wb.2 e:h12.5 e:wb.3 e:h12.6 f:dz.1 m:turn.26.27 d:outT.0 e:w3.0 m:turn.28 e:h12.7 f:bb.1
e:h12.8 f:bb.2 m:turn.29.30 e:wb.4 e:w3.1 m:turn.31 e:wb.5 m:turn.32 e:w3.2 m:turn.33 f:bb.3
"""
ACT_ORDER = """
d:silu.9 m:decay.0 d:wb.6 m:decay.1 d:silu.10.11 m:decay.2 m:bb.4 m:decay.3 m:bb.5 m:decay.4 d:wb.7
m:decay.5 d:wb.8 d:silu.12 m:wi_res.0 d:silu.13 d:wb.9 d:silu.14 m:bb.6 d:wb.10 d:silu.15 d:wb.11 m:wi_res.1
d:silu.16 d:wb.12 d:silu.17 m:bb.7 m:decay.6 m:bb.8 m:decay.7 e:x1T.0 m:decay.8 d:wb.13 m:decay.9.10 m:bb.9
m:decay.11 d:wb.14 m:decay.12 m:bb.10 e:gate_exp.0 d:silu.18 m:bb.11 d:silu.19 d:wb.15 d:silu.20 m:bb.12
d:silu.21 d:wb.16 d:silu.22 d:wb.17 m:decay.13 f:xT.0 m:decay.14 d:wb.18 d:silu.23 f:wi.0 m:bb.13.14 d:wb.19
e:silu.0 m:bb.15 d:wb.20 f:wi.1 e:silu.1 d:wb.21 m:decay.15 e:silu.2 e:wT.0 f:bT.0 e:wb.0 e:silu.3 f:bb.0
e:wb.1 e:silu.4 e:wb.2 e:silu.5 e:wb.3 e:silu.6 f:softplus.0 f:bb.1.2 e:wb.4 e:silu.7 e:wb.5 e:silu.8 f:bb.3
"""
DVE_ORDER = """
d:gated.8 m:c.0 e:yT.0 d:gated.9 m:scan.0 e:yT.1 m:scan.1 e:wo.0 m:ud.0 m:scan.2 d:gated.10 m:sum.0.1
d:gated.11 m:sum.2.3 m:scan.3 d:gated.12 m:sum.4 d:gated.13 m:sum.5 e:x1n.0 d:gated.14.15 m:sum.6 m:scan.4
m:sum.7 m:scan.5 m:sum.8 f:ln.0 m:sum.9.10 d:gated.16 m:scan.6 m:sum.11 e:gate.0 m:scan.7 d:gated.17
m:sum.12.13 d:gated.18 f:xn.0 d:gated.19 e:gate_w.0 d:gated.20.21 m:scan.8 m:sum.14 e:xsplit.0 m:sum.15
m:scan.9 m:sum.16.17 d:gated.22 m:sum.18.19 m:scan.10 d:gated.23 m:scan.11 e:gated.0 m:sum.20 m:scan.12
f:bc.0 m:sum.21.22 f:dz.0 e:gated.1 m:sum.23 e:gated.2 m:scan.13 m:sum.24 e:gated.3 d:eo.0 m:sum.25
e:gated.4 m:scan.14 e:gated.5.6 f:dz.1 m:sum.26.27 d:outT.0 m:scan.15 m:sum.28 f:delta.0 m:sum.29.30.31.32
e:gated.7 m:sum.33
"""
POOL_ORDER = """
m:du.0 d:weigh.4 m:dbu.0.1.2 d:weigh.5.6 m:xcur.0 m:dbu.3 e:rstd1.0 d:weigh.7.8.9 m:dbu.4 d:weigh.10.11
m:dbu.5.6 d:weigh.12.13 m:dbu.7 f:rstd.0 m:dbu.8.9 d:weigh.14.15.16.17 e:wsplit.0 m:dbu.10.11 d:weigh.18.19
m:dbu.12 d:weigh.20 m:dbu.13 f:bsplit.0 d:weigh.21 m:dbu.14 e:weigh.0.1.2 m:dbu.15 e:weigh.3 e:x1k.0
"""


def orders():
    steps = {}
    for engine, text in (("pe", PE_ORDER), ("act", ACT_ORDER), ("dve", DVE_ORDER), ("pool", POOL_ORDER)):
        steps[engine] = []
        for entry in text.split():
            part, step = entry.split(":")
            step, *args = step.split(".")
            steps[engine] += [(part, step, int(arg)) for arg in args]
    return steps


def mamba_moe_kernel(nc, x, w_in, w_delta, b_delta, w_b, w_c, a_log, d_param, w_out, wg_t, bias, w1_all,
                     w2_all, w3_all, sel_states, sel_experts, out):
    NT = x.shape[0] * x.shape[1] // TOK
    steps = orders()
    SIDE = ("xT", "wi", "wi_res", "dz", "bc", "bT", "bb", "yT", "wo", "x1T", "gate", "wT", "wb", "outT")

    SHIFT = {"f": 1, "m": 0, "e": -1, "d": -2}

    def body_parts(j):
        return "".join(part for part, shift in SHIFT.items() if 0 <= j + shift < NT)

    def side_uses(parts):
        return [(p, s, a) for p, s, a in steps["pe"] if s in SIDE and p in parts]

    def side_before(j):
        if isinstance(j, int):
            return sum(len(side_uses(body_parts(i))) for i in range(-1, j))
        per = len(side_uses("fmed"))
        return per * j + (side_before(2) - 2 * per)

    ctx = ExitStack()
    with ctx:
        def sb(name, shape, dt=F32):
            return ctx.enter_context(nc.sbuf_tensor(name, shape, dt))

        def bank(name):
            return ctx.enter_context(nc.psum_tensor(name, [P, 512], F32))

        def sem(name):
            return ctx.enter_context(nc.semaphore(name))

        ident = sb("ident", [P, P])
        ident_bf = sb("ident_bf", [P, P], BF16)
        sel_b = sb("sel_b", [3 * NS, NS, P], BF16)
        sel_w = sb("sel_w", [3 * E + 1, NK, P], BF16)
        before = sb("before", [P, E, E])
        half_exp = sb("half_exp", [P, TT])
        w_in_sb = sb("w_in_sb", [P, 2 * DI])
        w_delta_sb = sb("w_delta_sb", [P, NH, DI])
        w_bc_sb = sb("w_bc_sb", [P, NH, 2 * NS])
        w_out_sb = sb("w_out_sb", [P, NH, P])
        a_sb = sb("a_sb", [P, NH, NS])
        a_exp = sb("a_exp", [P, NH, NS])
        bd_sb = sb("bd_sb", [P, NH])
        dp_sb = sb("dp_sb", [P, NH])
        wg_sb = sb("wg_sb", [P, E])
        bias_sb = sb("bias_sb", [P, E])
        w1h = sb("w1h", [P, HIDDEN], F32R)
        w1l = sb("w1l", [P, HIDDEN], F32R)
        w2h = sb("w2h", [P, HIDDEN], F32R)
        w2l = sb("w2l", [P, HIDDEN], F32R)
        w3_sb = sb("w3_sb", [P, NK, P])
        x_in = sb("x_in", [P, TT, P])
        x_cur = sb("x_cur", [P, TT, P])
        xn = sb("xn", [P, TT, P])
        xnT = sb("xnT", [P, TOK])
        u = sb("u", [P, NH, TOK])
        sres = sb("sres", [P, NH, TOK])
        delta = sb("delta", [P, NH, TOK])
        y = sb("y", [P, NH, TOK])
        du = sb("du", [P, NH, TOK])
        bc = sb("bc", [P, TT, 2 * NS])
        c_sb = sb("c_sb", [P, TT, NS])
        bparts = sb("bparts", [P, TT, 3, NS], BF16)
        brest = sb("brest", [P, 2, TT, NS])
        bT = sb("bT", [3 * NS, TOK], BF16)
        bbc = sb("bbc", [P, BB_RING, TOK])
        decay = sb("decay", [P, DA_RING, GN, TOK])
        hb = sb("hb", [P, HB_RING, GN, TOK])
        acc = sb("acc", [P, TT, DI])
        one = sb("one", [P, 1])
        stats = {t: sb(f"stats_{t}", [P, TT, 6]) for t in ("x", "x1")}
        mv = {t: sb(f"mv_{t}", [P, TT, 2]) for t in ("x", "x1")}
        veps = {t: sb(f"veps_{t}", [P, TT]) for t in ("x", "x1")}
        rstd = {t: sb(f"rstd_{t}", [P, TT]) for t in ("x", "x1")}
        x1 = sb("x1", [P, TT, P])
        x1k = sb("x1k", [P, TT, P])
        x1n = xn
        x1nT = xnT
        xh = sb("xh", [P, TOK], F32R)
        xl = sb("xl", [P, TOK], F32R)
        g = sb("g", [P, TT, E])
        cmp_gt, cmp_ge = (y[:, i, 0:TT * E * E].rearrange("p (t e j) -> p t e j", t=TT, e=E) for i in range(2))
        rank = sb("rank", [P, TT, E])
        mask = sb("mask", [P, TT, E])
        gmax = sb("gmax", [P, TT])
        gm = sb("gm", [P, TT, E])
        gex = sb("gex", [P, TT, E])
        gem = sb("gem", [P, TT, E])
        gsum = sb("gsum", [P, TT])
        ginv = sb("ginv", [P, TT])
        w = sb("w", [P, TT, E])
        wparts = sb("wparts", [P, TT, 3, E], BF16)
        wrest = sb("wrest", [P, 2, TT, E])
        wT = sb("wT", [3 * E + 1, TOK], BF16)
        wbc = sb("wbc", [P, 2, TOK])
        s = sb("s", [P, S_RING, TOK])
        gated = sb("gated", [P, ACT_RING, TOK])
        stage = gated[:, :, :].rearrange("p a t -> p (a t)")[:, 0:HIDDEN]
        moe = sb("moe", [P, TOK])

        h1_bank = [bank(f"h1_{i}") for i in range(2)]
        h2_bank = [bank(f"h2_{i}") for i in range(2)]
        eo_bank = bank("eo_bank")
        turn_bank = [bank(f"turn_{i}") for i in range(2)]
        side = bank("side")
        side_bf = side[:, :].bitcast(BF16)

        consts = sem("consts")
        small_in = sem("small_in")
        w1_in, w2_in, w3_in = sem("w1_in"), sem("w2_in"), sem("w3_in")
        a_exped, a_ready = sem("a_exped"), sem("a_ready")
        w_hi, w_lo = sem("w_hi"), sem("w_lo")
        x_in_sem, out_stored = sem("x_in_sem"), sem("out_stored")
        ln_steps = {"x": sem("ln_steps_x"), "x1": sem("ln_steps_x1")}
        rstd_steps = {"x": sem("rstd_steps_x"), "x1": sem("rstd_steps_x1")}
        xn_ready = {"x": sem("xn_ready_x"), "x1": sem("xn_ready_x1")}
        x_cur_ready = sem("x_cur_ready")
        xnT_ready, wi_ready, sres_ready = sem("xnT_ready"), sem("wi_ready"), sem("sres_ready")
        side_full = sem("side_full")
        zb_ready, sp_steps, delta_ready, du_ready = sem("zb_ready"), sem("sp_steps"), sem("delta_ready"), sem("du_ready")
        bc_ready, bparts_steps, bT_ready, bb_ready = sem("bc_ready"), sem("bparts_steps"), sem("bT_ready"), sem("bb_ready")
        dbu_ready, decay_ready, scanned = sem("dbu_ready"), sem("decay_ready"), sem("scanned")
        turned, summed = sem("turned"), sem("summed")
        ud_ready, c_ready, y_ready = sem("ud_ready"), sem("c_ready"), sem("y_ready")
        x1_ready, x1k_ready, x1T_ready, xsplit = sem("x1_ready"), sem("x1k_ready"), sem("x1T_ready"), sem("xsplit")
        gate_steps, gex_ready, wparts_steps, wT_ready, wbc_ready = (
            sem("gate_steps"), sem("gex_ready"), sem("wparts_steps"), sem("wT_ready"), sem("wbc_ready"))
        h1_full, h2_full, s_ready, gated_ready = sem("h1_full"), sem("h2_full"), sem("s_ready"), sem("gated_ready")
        weighed, w3_done, eo_done, out_ready = sem("weighed"), sem("w3_done"), sem("eo_done"), sem("out_ready")

        x_t = x.rearrange("b (c p) d -> p (b c) d", p=P)
        out_t = out.rearrange("b (c p) d -> p (b c) d", p=P)

        def count(turn, per, c):
            j, shift = turn
            return per * j + (per * shift + c)

        def wait_before(eng, s_, turn, per, c):
            value = count(turn, per, c)
            if isinstance(value, int):
                if value <= 0:
                    return
            else:
                assert per * (2 + turn[1]) + c > 0
            eng.wait_ge(s_, value)

        def carry_waits(eng):
            eng.nop(nofuse=True)

        def bodies(eng, program):
            for j in range(-1, 2):
                program(j, body_parts(j))
            with eng.Fori(2, NT - 1) as j:
                program(j, "fmed")
            for j in range(NT - 1, NT + 2):
                program(j, body_parts(j))

        def turn_of(j, part):
            return (j, SHIFT[part])

        def side_index(j, parts, part, step, arg):
            return side_uses(parts).index((part, step, arg)) + 1 + side_before(j)

        def turned_before(grp):
            last = grp - HB_RING // NH
            return 2 + 2 * GN * (last + 1) if last >= 0 else 2 * GN * (last + 1)

        def tile_rows(k):
            return min(P, HIDDEN - k * P)

        def hidden_ring(k):
            return k - 2

        SMALL = 12
        CONSTS = 9
        FILLS = 2 * (NS + 1)
        SUMS = 2 * FILLS
        block = ctx.enter_context(nc.Block())

        @block.sync
        def _(sp_eng):
            def load_x(turn):
                wait_before(sp_eng, xn_ready["x"], turn, TT, 0)
                carry_waits(sp_eng)
                wait_before(sp_eng, x_cur_ready, turn, 1, 0)
                at = TT * turn[0] + TT * turn[1]
                carry_waits(sp_eng)
                sp_eng.dma_start(x_in[:, :, :], x_t[:, bass.ds(at, TT), :]).then_inc(x_in_sem, 16)

            def load_weights():
                small = [(w_in_sb[:, :], w_in), (w_delta_sb[:, :, :], w_delta.rearrange("(k p) n -> p k n", p=P)),
                         (w_bc_sb[:, :, 0:NS], w_b.rearrange("(k p) n -> p k n", p=P)),
                         (w_bc_sb[:, :, NS:], w_c.rearrange("(k p) n -> p k n", p=P)),
                         (w_out_sb[:, :, :], w_out.rearrange("(k p) n -> p k n", p=P)),
                         (a_sb[:, :, :], a_log.rearrange("(k p) n -> p k n", p=P)),
                         (bd_sb[:, :], b_delta),
                         (dp_sb[:, :], d_param),
                         (wg_sb[:, :], wg_t), (bias_sb[:, :], bias.partition_broadcast(P)),
                         (sel_b[:, :, :].bitcast(U16), sel_states), (sel_w[:, :, :].bitcast(U16), sel_experts)]
                for dst, src in small:
                    sp_eng.dma_start(dst, src).then_inc(small_in, 16)
                assert len(small) == SMALL
                sp_eng.dma_start(stage, w1_all).then_inc(w1_in, 16)
                full = HIDDEN // P
                sp_eng.dma_start(w3_sb[:, 0:full, :], w3_all[0:full * P, :].rearrange("(t p) d -> p t d", p=P))\
                    .then_inc(w3_in, 16)
                sp_eng.dma_start(w3_sb[0:HIDDEN - full * P, full, :], w3_all[full * P:, :]).then_inc(w3_in, 16)

            def load_w2():
                sp_eng.wait_ge(w_lo, 1)
                sp_eng.dma_start(stage, w2_all).then_inc(w2_in, 16)

            def program(j, parts):
                if "f" in parts:
                    load_x(turn_of(j, "f"))
                if isinstance(j, int) and j == -1:
                    load_weights()
                if isinstance(j, int) and j == 0:
                    load_w2()
                if "d" in parts:
                    sp_eng.wait_ge(out_ready, count(turn_of(j, "d"), 1, 1))
                    at = TT * j + TT * SHIFT["d"]
                    carry_waits(sp_eng)
                    sp_eng.dma_start(out_t[:, bass.ds(at, TT), :], x1k[:, :, :]).then_inc(out_stored, 16)

            bodies(sp_eng, program)
            sp_eng.wait_ge(out_stored, 16 * NT)

        @block.gpsimd
        def _(pool):
            pool.memset(ident[:, :], 0.0).then_inc(consts, 1)
            pool.memset(before[:, :, :], 1.0).then_inc(consts, 1)
            pool.wait_ge(consts, 2)
            pool.affine_select(out=ident[:, :], in_=ident[:, :], compare_op=ALU.not_equal, fill=1.0, base=0,
                               pattern=[[-1, P]], channel_multiplier=1).then_inc(consts, 1)
            pool.affine_select(out=before[:, :, :], in_=before[:, :, :], compare_op=ALU.is_ge, fill=0.0, base=-1,
                               pattern=[[1, E], [-1, E]], channel_multiplier=0).then_inc(consts, 1)
            pool.wait_ge(consts, 4)
            pool.tensor_copy(ident_bf[:, :], ident[:, :]).then_inc(consts, 1)
            pool.memset(half_exp[:, :], -0.5).then_inc(consts, 1)
            pool.memset(one[:, :], 1.0).then_inc(consts, 1)
            pool.memset(wT[:, :], 1.0).then_inc(consts, 1)
            pool.memset(decay[:, :, :, :].rearrange("p r n (b t) -> p (r n b) t", t=SEQ)[:, :, 0:1], 0.0).then_inc(consts, 1)

            def take_rstd(norm, turn):
                pool.wait_ge(ln_steps[norm], count(turn, 2 * TT, 2 * TT))
                wait_before(pool, xn_ready[norm], turn, TT, 0)
                carry_waits(pool)
                pool.tensor_scalar(veps[norm][:, :], mv[norm][:, :, 1], EPS, 1.0, ALU.add, ALU.mult)\
                    .then_inc(rstd_steps[norm], 1)
                pool.wait_ge(rstd_steps[norm], count(turn, 2, 1))
                pool.tensor_tensor(rstd[norm][:, :], veps[norm][:, :], half_exp[:, :], ALU.pow)\
                    .then_inc(rstd_steps[norm], 1)

            def cut(parts_tile, rest, src, steps_sem, turn):
                for i in range(3):
                    cur = src if i == 0 else rest[:, i - 1]
                    if i:
                        pool.wait_ge(steps_sem, count(turn, 5, 2 * i))
                    carry_waits(pool)
                    pool.tensor_copy(parts_tile[:, :, i, :], cur).then_inc(steps_sem, 1)
                    if i < 2:
                        pool.wait_ge(steps_sem, count(turn, 5, 2 * i + 1))
                        pool.tensor_tensor(rest[:, i], cur, parts_tile[:, :, i, :], ALU.subtract)\
                            .then_inc(steps_sem, 1)

            def program(j, parts):
                for part, step, arg in steps["pool"]:
                    if part not in parts:
                        continue
                    turn = turn_of(j, part)
                    if step == "bsplit":
                        pool.wait_ge(bc_ready, count(turn, 1, 1))
                        wait_before(pool, bT_ready, turn, 1, 0)
                        cut(bparts, brest, bc[:, :, 0:NS], bparts_steps, turn)
                    elif step == "du":
                        pool.wait_ge(delta_ready, count(turn, 1, 1))
                        wait_before(pool, dbu_ready, turn, NU, 0)
                        pool.tensor_tensor(du[:, :, :], delta[:, :, :], u[:, :, :], ALU.mult).then_inc(du_ready, 1)
                    elif step == "dbu":
                        grp, h = divmod(arg, NH)
                        pool.wait_ge(du_ready, count(turn, 1, 1))
                        pool.wait_ge(bb_ready, count(turn, NS, GN * grp + GN))
                        wait_before(pool, turned, turn, FILLS, turned_before(grp))
                        r = GN * grp % BB_RING
                        pool.tensor_tensor(hb[:, arg % HB_RING, :, :],
                                           du[:, h, :].unsqueeze(1).broadcast_to((P, GN, TOK)),
                                           bbc[:, r:r + GN, :], ALU.mult).then_inc(dbu_ready, 1)
                    elif step == "rstd1":
                        take_rstd("x1", turn)
                    elif step == "rstd":
                        take_rstd("x", turn)
                    elif step == "wsplit":
                        pool.wait_ge(gate_steps, count(turn, GATE_STEPS, GATE_STEPS))
                        wait_before(pool, wT_ready, turn, 1, 0)
                        cut(wparts, wrest, w[:, :, :], wparts_steps, turn)
                    elif step == "x1k":
                        pool.wait_ge(x1_ready, count(turn, 1, 1))
                        wait_before(pool, out_stored, turn, 16, 0)
                        carry_waits(pool)
                        pool.tensor_copy(x1k[:, :, :], x1[:, :, :]).then_inc(x1k_ready, 1)
                    elif step == "xcur":
                        pool.wait_ge(x_in_sem, count(turn, 16, 16))
                        wait_before(pool, x1_ready, turn, 1, 0)
                        carry_waits(pool)
                        pool.tensor_copy(x_cur[:, :, :], x_in[:, :, :]).then_inc(x_cur_ready, 1)
                    elif step == "weigh":
                        k = K_ONE + arg
                        rows = tile_rows(k)
                        pool.wait_ge(gated_ready, count(turn, NK, k + 1))
                        pool.wait_ge(wbc_ready, count(turn, NW, arg + 1))
                        tile = gated[0:rows, k % ACT_RING, :]
                        pool.tensor_tensor(tile, tile, wbc[0:rows, arg % 2, :], ALU.mult).then_inc(weighed, 1)

            bodies(pool, program)

        @block.scalar
        def _(act):
            def read_side(j, parts, part, step, arg, out_ap, in_ap, func, ready):
                act.wait_ge(side_full, side_index(j, parts, part, step, arg))
                act.activation(out_ap, in_ap, func).then_inc(ready, 1)

            def program(j, parts):
                for part, step, arg in steps["act"]:
                    if part not in parts:
                        continue
                    turn = turn_of(j, part)
                    if step == "x1T":
                        read_side(j, parts, part, step, arg, x1nT[:, :], side[:, :], ACT.Copy, x1T_ready)
                    elif step == "softplus":
                        act.preload_act_table_set("natural_log_exp_and_others")
                        act.wait_ge(zb_ready, count(turn, NH, NH))
                        wait_before(act, dbu_ready, turn, NU, 0)
                        act.activation(du[:, :, :], delta[:, :, :], ACT.Abs).then_inc(sp_steps, 1)
                        act.wait_ge(sp_steps, count(turn, 3, 1))
                        act.activation(du[:, :, :], du[:, :, :], ACT.Exp, scale=-1.0).then_inc(sp_steps, 1)
                        act.wait_ge(sp_steps, count(turn, 3, 2))
                        act.activation(du[:, :, :], du[:, :, :], ACT.Ln, bias=one[:, :]).then_inc(sp_steps, 1)
                    elif step == "bT":
                        read_side(j, parts, part, step, arg, bT[:, :], side_bf[0:3 * NS, 0:TOK], ACT.Copy, bT_ready)
                    elif step == "bb":
                        wait_before(act, dbu_ready, turn, NU, NH * ((arg - BB_RING) // GN + 1))
                        read_side(j, parts, part, step, arg, bbc[:, arg % BB_RING, :], side[:, :], ACT.Copy, bb_ready)
                    elif step == "decay":
                        grp, h = divmod(arg, NH)
                        act.wait_ge(delta_ready, count(turn, 1, 1))
                        wait_before(act, scanned, turn, NU, arg - DA_RING + 1)
                        for i in range(GN):
                            act.activation(
                                decay[:, arg % DA_RING, i, :].rearrange("p (b t) -> p b t", t=SEQ)[:, :, 1:],
                                delta[:, h, :].rearrange("p (b t) -> p b t", t=SEQ)[:, :, 1:],
                                ACT.Exp, scale=a_sb[:, h, GN * grp + i:GN * grp + i + 1]).then_inc(decay_ready, 1)
                    elif step == "gate_exp":
                        act.wait_ge(gate_steps, count(turn, GATE_STEPS, 9))
                        act.activation(gex[:, :, :], gm[:, :, :], ACT.Exp).then_inc(gex_ready, 1)
                    elif step == "wT":
                        read_side(j, parts, part, step, arg, wT[0:3 * E, :], side_bf[0:3 * E, 0:TOK], ACT.Copy, wT_ready)
                    elif step == "wb":
                        wait_before(act, weighed, turn, NW, arg - 1)
                        read_side(j, parts, part, step, arg, wbc[:, arg % 2, :], side[:, :], ACT.Copy, wbc_ready)
                    elif step == "silu":
                        rows = tile_rows(arg)
                        act.wait_ge(h1_full, count(turn, NK, arg + 1))
                        wait_before(act, gated_ready, turn, NK, arg - S_RING + 1)
                        act.activation(s[0:rows, arg % S_RING, :], h1_bank[arg % 2][0:rows, :], ACT.Silu)\
                           .then_inc(s_ready, 1)
                    elif step == "xT":
                        wait_before(act, xsplit, turn, 2, -2)
                        wait_before(act, gate_steps, turn, GATE_STEPS, -GATE_STEPS)
                        read_side(j, parts, part, step, arg, xnT[:, :], side[:, :], ACT.Copy, xnT_ready)
                    elif step == "wi":
                        wait_before(act, du_ready, turn, 1, 0)
                        wait_before(act, turned, turn, FILLS, 2 - FILLS)
                        read_side(j, parts, part, step, arg, u[:, arg, :], side[:, :], ACT.Silu, wi_ready)
                    elif step == "wi_res":
                        wait_before(act, y_ready, turn, NH, 0)
                        read_side(j, parts, part, step, arg, sres[:, arg, :], side[:, :], ACT.Silu, sres_ready)
                    if isinstance(j, int) and j + SHIFT[part] == 0 and step == "decay" and arg in (4, 10):
                        cut_hi(arg == 10)

            def cut_hi(second):
                act.wait_ge(w2_in if second else w1_in, 16)
                dst = w2h if second else w1h
                act.activation(dst[:, :], stage, ACT.Copy).then_inc(w_hi, 1)

            act.wait_ge(small_in, 16 * SMALL)
            act.activation(a_exp[:, :, :], a_sb[:, :, :], ACT.Exp).then_inc(a_exped, 1)
            act.wait_ge(consts, CONSTS)
            act.wait_ge(a_ready, 1)
            bodies(act, program)

        @block.vector
        def _(dve):
            def take_stats(norm, src, turn):
                for i in range(TT):
                    dve.bn_stats(stats[norm][:, i, :], src[:, i, :]).then_inc(ln_steps[norm], 1)
                for i in range(TT):
                    dve.wait_ge(ln_steps[norm], count(turn, 2 * TT, i + 1))
                    carry_waits(dve)
                    dve.bn_aggr(mv[norm][:, i, :], stats[norm][:, i, :]).then_inc(ln_steps[norm], 1)

            def normalize(norm, src, dst, turn):
                dve.wait_ge(rstd_steps[norm], count(turn, 2, 2))
                for i in range(TT):
                    dve.tensor_scalar(dst[:, i, :], src[:, i, :], mv[norm][:, i, 0:1], rstd[norm][:, i:i + 1],
                                      ALU.subtract, ALU.mult).then_inc(xn_ready[norm], 1)

            def side_wait(j, parts, part, step, arg):
                dve.wait_ge(side_full, side_index(j, parts, part, step, arg))

            def cut_lo(second):
                dve.wait_ge(w_hi, 2 if second else 1)
                hi, lo = (w2h, w2l) if second else (w1h, w1l)
                dve.tensor_tensor(lo[:, :], stage, hi[:, :].bitcast(F32), ALU.subtract).then_inc(w_lo, 1)

            def program(j, parts):
                for part, step, arg in steps["dve"]:
                    if part not in parts:
                        continue
                    turn = turn_of(j, part)
                    if step == "dz":
                        wait_before(dve, decay_ready, turn, NS * NH, 0)
                        wait_before(dve, du_ready, turn, 1, 0)
                        side_wait(j, parts, part, "dz", arg)
                        dve.tensor_scalar(delta[:, arg, :], side[:, :], bd_sb[:, arg:arg + 1], None, ALU.add)\
                           .then_inc(zb_ready, 1)
                    elif step == "bc":
                        wait_before(dve, bparts_steps, turn, 5, 0)
                        wait_before(dve, c_ready, turn, 1, 0)
                        side_wait(j, parts, part, "bc", 0)
                        dve.tensor_copy(bc[:, :, :], side[:, 0:TT * 2 * NS].rearrange("p (t n) -> p t n", t=TT))\
                           .then_inc(bc_ready, 1)
                    elif step == "delta":
                        dve.wait_ge(sp_steps, count(turn, 3, 3))
                        dve.scalar_tensor_tensor(delta[:, :, :], delta[:, :, :], 0.0, du[:, :, :], ALU.max, ALU.add)\
                           .then_inc(delta_ready, 1)
                    elif step == "scan":
                        dve.wait_ge(decay_ready, count(turn, NS * NH, GN * (arg + 1)))
                        dve.wait_ge(dbu_ready, count(turn, NU, arg + 1))
                        states = hb[:, arg % HB_RING, :, :].rearrange("p n t -> p (n t)")
                        dve.tensor_tensor_scan(states,
                                               decay[:, arg % DA_RING, :, :].rearrange("p n t -> p (n t)"),
                                               states, 0.0, ALU.mult, ALU.add).then_inc(scanned, 1)
                    elif step == "c":
                        dve.wait_ge(bc_ready, count(turn, 1, 1))
                        wait_before(dve, summed, turn, SUMS, 0)
                        dve.tensor_copy(c_sb[:, :, :], bc[:, :, NS:]).then_inc(c_ready, 1)
                    elif step == "ud":
                        dve.wait_ge(wi_ready, count(turn, NH, NH))
                        for h in range(NH):
                            dve.tensor_scalar(y[:, h, :], u[:, h, :], dp_sb[:, h:h + 1], None, ALU.mult)\
                               .then_inc(ud_ready, 1)
                    elif step == "sum":
                        n, pair = arg // 2 - 1, arg % 2
                        dve.wait_ge(turned, count(turn, FILLS, arg + 1))
                        if n == 0:
                            dve.wait_ge(c_ready, count(turn, 1, 1))
                        if n >= 0:
                            dve.wait_ge(summed, count(turn, SUMS, 2 * arg - 2))
                        for i in range(2):
                            blk = 2 * pair + i
                            hT = turn_bank[pair][:, i * DI:(i + 1) * DI]
                            if n >= 0:
                                ins = dve.scalar_tensor_tensor(acc[:, blk, :], hT, c_sb[:, blk, n:n + 1], acc[:, blk, :],
                                                               ALU.mult, ALU.add)
                            else:
                                ins = dve.tensor_copy(acc[:, blk, :], hT)
                            ins.then_inc(summed, 1)
                    elif step == "yT":
                        dve.wait_ge(sres_ready, count(turn, NH, NH))
                        side_wait(j, parts, part, "yT", arg)
                        dve.tensor_tensor(y[:, arg, :], side[:, :], sres[:, arg, :], ALU.mult).then_inc(y_ready, 1)
                    elif step == "wo":
                        dve.wait_ge(x_cur_ready, count(turn, 1, 1))
                        wait_before(dve, x1k_ready, turn, 1, 0)
                        wait_before(dve, xn_ready["x1"], turn, TT, 0)
                        side_wait(j, parts, part, "wo", 0)
                        dve.tensor_tensor(x1[:, :, :], side[:, :].rearrange("p (t d) -> p t d", t=TT), x_cur[:, :, :],
                                          ALU.add).then_inc(x1_ready, 1)
                        dve.wait_ge(x1_ready, count(turn, 1, 1))
                        take_stats("x1", x1, turn)
                    elif step == "x1n":
                        if not (isinstance(j, int) and j + SHIFT[part] == NT - 1):
                            dve.wait_ge(xnT_ready, count(turn, 1, 2))
                        normalize("x1", x1, x1n, turn)
                    elif step == "gate":
                        def then(c, ins):
                            ins.then_inc(gate_steps, 1)
                            dve.wait_ge(gate_steps, count(turn, GATE_STEPS, c))

                        side_wait(j, parts, part, "gate", 0)
                        then(1, dve.tensor_tensor(g[:, :, :], side[:, 0:TT * E].rearrange("p (t e) -> p t e", t=TT),
                                                  bias_sb[:, :].unsqueeze(1).broadcast_to((P, TT, E)), ALU.add))
                        gj = g[:, :, :].unsqueeze(2).broadcast_to((P, TT, E, E))
                        ge = g[:, :, :].unsqueeze(3).broadcast_to((P, TT, E, E))
                        then(2, dve.tensor_tensor(cmp_gt[:, :, :, :], gj, ge, ALU.is_gt))
                        then(3, dve.tensor_tensor(cmp_ge[:, :, :, :], gj, ge, ALU.is_ge))
                        then(4, dve.tensor_tensor(cmp_ge[:, :, :, :], cmp_ge[:, :, :, :],
                                                  before[:, :, :].unsqueeze(1).broadcast_to((P, TT, E, E)), ALU.mult))
                        then(5, dve.tensor_tensor(cmp_gt[:, :, :, :], cmp_gt[:, :, :, :], cmp_ge[:, :, :, :], ALU.max))
                        then(6, dve.tensor_reduce(rank[:, :, :], cmp_gt[:, :, :, :], AX.X, ALU.add))
                        then(7, dve.tensor_scalar(mask[:, :, :], rank[:, :, :], TOPK - 0.5, None, ALU.is_lt))
                        then(8, dve.tensor_reduce(gmax[:, :], g[:, :, :], AX.X, ALU.max))
                        then(9, dve.tensor_tensor(gm[:, :, :], g[:, :, :],
                                                  gmax[:, :].unsqueeze(2).broadcast_to((P, TT, E)), ALU.subtract))
                    elif step == "gate_w":
                        def then(c, ins):
                            ins.then_inc(gate_steps, 1)
                            dve.wait_ge(gate_steps, count(turn, GATE_STEPS, c))

                        dve.wait_ge(gex_ready, count(turn, 1, 1))
                        wait_before(dve, wparts_steps, turn, 5, 0)
                        then(10, dve.tensor_tensor(gem[:, :, :], gex[:, :, :], mask[:, :, :], ALU.mult))
                        then(11, dve.tensor_reduce(gsum[:, :], gem[:, :, :], AX.X, ALU.add))
                        then(12, dve.reciprocal(ginv[:, :], gsum[:, :]))
                        then(13, dve.tensor_tensor(w[:, :, :], gem[:, :, :],
                                                   ginv[:, :].unsqueeze(2).broadcast_to((P, TT, E)), ALU.mult))
                    elif step == "gated":
                        rows = tile_rows(arg)
                        dve.wait_ge(h2_full, count(turn, NK, arg + 1))
                        dve.wait_ge(s_ready, count(turn, NK, arg + 1))
                        wait_before(dve, w3_done, turn, NK, arg - ACT_RING + 1)
                        dve.tensor_tensor(gated[0:rows, arg % ACT_RING, :], h2_bank[arg % 2][0:rows, :],
                                          s[0:rows, arg % S_RING, :], ALU.mult).then_inc(gated_ready, 1)
                    elif step == "eo":
                        dve.wait_ge(w3_done, count(turn, NK, NK))
                        dve.tensor_copy(moe[:, :], eo_bank[:, :]).then_inc(eo_done, 1)
                    elif step == "outT":
                        dve.wait_ge(x1k_ready, count(turn, 1, 1))
                        side_wait(j, parts, part, "outT", 0)
                        dve.tensor_tensor(x1k[:, :, :], side[:, :].rearrange("p (t d) -> p t d", t=TT), x1k[:, :, :],
                                          ALU.add).then_inc(out_ready, 1)
                    elif step == "xsplit":
                        dve.wait_ge(x1T_ready, count(turn, 1, 1))
                        wait_before(dve, h2_full, turn, NK, 0)
                        dve.tensor_copy(xh[:, :], x1nT[:, :]).then_inc(xsplit, 1)
                        dve.wait_ge(xsplit, count(turn, 2, 1))
                        dve.tensor_tensor(xl[:, :], x1nT[:, :], xh[:, :].bitcast(F32), ALU.subtract).then_inc(xsplit, 1)
                    elif step == "ln":
                        dve.wait_ge(x_in_sem, count(turn, 16, 16))
                        take_stats("x", x_in, turn)
                    elif step == "xn":
                        wait_before(dve, x1T_ready, turn, 1, -1)
                        normalize("x", x_in, xn, turn)
                    if isinstance(j, int) and j + SHIFT[part] == 0 and step == "scan" and arg in (4, 10):
                        cut_lo(arg == 10)

            dve.wait_ge(a_exped, 1)
            dve.tensor_scalar(a_sb[:, :, :], a_exp[:, :, :], -1.0, None, ALU.mult).then_inc(a_ready, 1)
            dve.wait_ge(consts, CONSTS)
            bodies(dve, program)

        @block.tensor
        def _(pe):
            SIDE_READ = {"xT": (xnT_ready, 1), "wi": (wi_ready, NH), "wi_res": (sres_ready, NH), "dz": (zb_ready, NH),
                         "bc": (bc_ready, 1), "bT": (bT_ready, 1), "bb": (bb_ready, NS), "yT": (y_ready, NH),
                         "wo": (x1_ready, 1), "x1T": (x1T_ready, 1), "gate": (gate_steps, GATE_STEPS),
                         "wT": (wT_ready, 1), "wb": (wbc_ready, NW), "outT": (out_ready, 1)}

            def side_free(j, parts, part, step, arg):
                uses = side_uses(parts)
                n = uses.index((part, step, arg))
                if n:
                    last_part, last_step, last_arg = uses[n - 1]
                    turn = turn_of(j, last_part)
                elif isinstance(j, int) and j == -1:
                    return
                else:
                    uses = side_uses(body_parts(j - 1) if isinstance(j, int) else "fmed")
                    last_part, last_step, last_arg = uses[-1]
                    turn = (j, SHIFT[last_part] - 1)
                reader, per = SIDE_READ[last_step]
                wait_before(pe, reader, turn, per, last_arg + 1)

            def program(j, parts):
                for part, step, arg in steps["pe"]:
                    if part not in parts:
                        continue
                    turn = turn_of(j, part)
                    if step == "x1T":
                        pe.wait_ge(xn_ready["x1"], count(turn, TT, TT))
                        side_free(j, parts, part, step, arg)
                        for i in range(TT):
                            mm = pe.transpose(side[:, i * P:(i + 1) * P], x1n[:, i, :], ident[:, :])
                        mm.then_inc(side_full, 1)
                    elif step == "dz":
                        pe.wait_ge(wi_ready, count(turn, NH, NH))
                        side_free(j, parts, part, step, arg)
                        for k in range(NH):
                            mm = pe.matmul(side[:, :], w_delta_sb[:, k, arg * P:(arg + 1) * P], u[:, k, :],
                                           start=(k == 0), stop=(k == NH - 1))
                        mm.then_inc(side_full, 1)
                    elif step == "bc":
                        pe.wait_ge(wi_ready, count(turn, NH, NH))
                        side_free(j, parts, part, step, arg)
                        for i in range(TT):
                            for k in range(NH):
                                mm = pe.matmul(side[:, i * 2 * NS:(i + 1) * 2 * NS], u[:, k, i * P:(i + 1) * P],
                                               w_bc_sb[:, k, :], start=(k == 0), stop=(k == NH - 1))
                        mm.then_inc(side_full, 1)
                    elif step == "gate":
                        pe.wait_ge(x1T_ready, count(turn, 1, 1))
                        side_free(j, parts, part, step, arg)
                        for i in range(TT):
                            mm = pe.matmul(side[:, i * E:(i + 1) * E], x1nT[:, i * P:(i + 1) * P], wg_sb[:, :],
                                           start=True, stop=True)
                        mm.then_inc(side_full, 1)
                    elif step == "bT":
                        pe.wait_ge(bparts_steps, count(turn, 5, 5))
                        side_free(j, parts, part, step, arg)
                        carry_waits(pe)
                        for i in range(TT):
                            mm = pe.transpose(side_bf[0:3 * NS, i * P:(i + 1) * P],
                                              bparts[:, i, :, :].rearrange("p c n -> p (c n)"), ident_bf[:, :])
                        mm.then_inc(side_full, 1)
                    elif step == "bb":
                        pe.wait_ge(bT_ready, count(turn, 1, 1))
                        side_free(j, parts, part, step, arg)
                        pe.matmul(side[:, :], sel_b[:, arg, :], bT[:, :], start=True, stop=True).then_inc(side_full, 1)
                    elif step == "wT":
                        pe.wait_ge(wparts_steps, count(turn, 5, 5))
                        side_free(j, parts, part, step, arg)
                        carry_waits(pe)
                        for i in range(TT):
                            mm = pe.transpose(side_bf[0:3 * E, i * P:(i + 1) * P],
                                              wparts[:, i, :, :].rearrange("p c n -> p (c n)"), ident_bf[:, :])
                        mm.then_inc(side_full, 1)
                    elif step == "wb":
                        pe.wait_ge(wT_ready, count(turn, 1, 1))
                        side_free(j, parts, part, step, arg)
                        pe.matmul(side[:, :], sel_w[:, K_ONE + arg, :], wT[:, :], start=True, stop=True).then_inc(side_full, 1)
                    elif step == "turn":
                        n, pair = arg // 2 - 1, arg % 2
                        grp, i_n = divmod(n, GN)
                        if n < 0:
                            pe.wait_ge(ud_ready, count(turn, NH, NH))
                        else:
                            pe.wait_ge(scanned, count(turn, NU, NH * (grp + 1)))
                        wait_before(pe, summed, turn, SUMS, 2 * arg - 2)
                        for i in range(2):
                            blk = 2 * pair + i
                            for h in range(NH):
                                src = y[:, h, :] if n < 0 else hb[:, (NH * grp + h) % HB_RING, i_n, :]
                                mm = pe.transpose(turn_bank[pair][:, (NH * i + h) * P:(NH * i + h + 1) * P],
                                                  src[:, blk * P:(blk + 1) * P], ident[:, :])
                        mm.then_inc(turned, 1)
                    elif step == "yT":
                        pe.wait_ge(summed, count(turn, SUMS, SUMS))
                        side_free(j, parts, part, step, arg)
                        for i in range(TT):
                            mm = pe.transpose(side[:, i * P:(i + 1) * P], acc[:, i, arg * P:(arg + 1) * P], ident[:, :])
                        mm.then_inc(side_full, 1)
                    elif step == "wo":
                        pe.wait_ge(y_ready, count(turn, NH, NH))
                        side_free(j, parts, part, step, arg)
                        for i in range(TT):
                            for k in range(NH):
                                mm = pe.matmul(side[:, i * P:(i + 1) * P], y[:, k, i * P:(i + 1) * P], w_out_sb[:, k, :],
                                               start=(k == 0), stop=(k == NH - 1))
                        mm.then_inc(side_full, 1)
                    elif step == "h12":
                        rows = tile_rows(arg)
                        cols = slice(arg * P, arg * P + rows)
                        if arg == 0:
                            pe.wait_ge(xsplit, count(turn, 2, 2))
                            if isinstance(j, int) and j == 1:
                                pe.wait_ge(w_lo, 2)
                        for banks, hi, lo, free, full in ((h1_bank, w1h, w1l, s_ready, h1_full),
                                                          (h2_bank, w2h, w2l, gated_ready, h2_full)):
                            wait_before(pe, free, turn, NK, hidden_ring(arg) + 1)
                            dst = banks[arg % 2][0:rows, :]
                            pe.matmul(dst, hi[:, cols], xh[:, :], start=True, stop=False)
                            pe.matmul(dst, hi[:, cols], xl[:, :], start=False, stop=False)
                            pe.matmul(dst, lo[:, cols], xh[:, :], start=False, stop=True).then_inc(full, 1)
                    elif step == "w3":
                        rows = tile_rows(arg)
                        if isinstance(j, int) and j == 1 and arg == 0:
                            pe.wait_ge(w3_in, 32)
                        if arg < K_ONE:
                            pe.wait_ge(gated_ready, count(turn, NK, arg + 1))
                        else:
                            pe.wait_ge(weighed, count(turn, NW, arg - K_ONE + 1))
                        if arg == 0:
                            wait_before(pe, eo_done, turn, 1, 0)
                        pe.matmul(eo_bank[:, :], w3_sb[0:rows, arg, :], gated[0:rows, arg % ACT_RING, :],
                                  start=(arg == 0), stop=(arg == NK - 1)).then_inc(w3_done, 1)
                    elif step == "outT":
                        pe.wait_ge(eo_done, count(turn, 1, 1))
                        side_free(j, parts, part, step, arg)
                        for i in range(TT):
                            mm = pe.transpose(side[:, i * P:(i + 1) * P], moe[:, i * P:(i + 1) * P], ident[:, :])
                        mm.then_inc(side_full, 1)
                    elif step == "xT":
                        pe.wait_ge(xn_ready["x"], count(turn, TT, TT))
                        side_free(j, parts, part, step, arg)
                        for i in range(TT):
                            mm = pe.transpose(side[:, i * P:(i + 1) * P], xn[:, i, :], ident[:, :])
                        mm.then_inc(side_full, 1)
                    elif step in ("wi", "wi_res"):
                        pe.wait_ge(xnT_ready, count(turn, 1, 1))
                        side_free(j, parts, part, step, arg)
                        tile = arg + (NH if step == "wi_res" else 0)
                        pe.matmul(side[:, :], w_in_sb[:, tile * P:(tile + 1) * P], xnT[:, :], start=True, stop=True)\
                          .then_inc(side_full, 1)

            pe.wait_ge(consts, CONSTS)
            pe.wait_ge(small_in, 16 * SMALL)
            bodies(pe, program)


def kernel(**inputs):
    import numpy as np
    import concourse.bacc as _bacc
    from concourse import mybir as _mybir
    from concourse.bass_utils import run_bass_kernel_spmd as _run

    a = {k: np.asarray(v) for k, v in inputs.items()}

    def join(name):
        return np.concatenate([a["L0_ffn_Ws" + name[1]], a["L0_ffn_" + name].reshape(E * HID, P)])

    one = 0x3F80
    sel_states = np.zeros((3 * NS, NS, P), np.uint16)
    sel_experts = np.zeros((3 * E + 1, NK * P), np.uint16)
    for part in range(3):
        for n in range(NS):
            sel_states[NS * part + n, n] = one
        for e in range(E):
            sel_experts[E * part + e, HID * (e + 1):HID * (e + 2)] = one
    sel_experts[3 * E, 0:HID] = one
    sel_experts = sel_experts.reshape(3 * E + 1, NK, P)
    laid = {
        "x": a["L0_attn_x"], "w_in": a["L0_attn_W_in"], "w_delta": a["L0_attn_W_delta"],
        "b_delta": a["L0_attn_b_delta"].reshape(NH, P).T, "w_b": a["L0_attn_W_B"], "w_c": a["L0_attn_W_C"],
        "a_log": a["L0_attn_A_log"], "d_param": a["L0_attn_D_param"].reshape(NH, P).T, "w_out": a["L0_attn_W_out"],
        "wg_t": a["L0_ffn_Wg"].T, "bias": a["L0_ffn_routing_bias"],
        "w1_all": join("W1").T, "w2_all": join("W2").T,
        "w3_all": np.concatenate([a["L0_ffn_Ws3"].T, a["L0_ffn_W3"].transpose(0, 2, 1).reshape(E * HID, P)]),
        "sel_states": sel_states, "sel_experts": sel_experts,
    }
    nc = _bacc.Bacc("TRN2", target_bir_lowering=False, num_devices=1)
    arrays, args = {}, []
    for name, v in laid.items():
        v = np.ascontiguousarray(v)
        arrays[f"{name}_dram"] = v
        args.append(nc.dram_tensor(f"{name}_dram", v.shape, _mybir.dt.from_np(v.dtype), kind="ExternalInput").ap())
    args.append(nc.dram_tensor("out_dram", laid["x"].shape, _mybir.dt.float32, kind="ExternalOutput").ap())
    mamba_moe_kernel(nc, *args)
    r = _run(nc, [arrays], core_ids=[0])
    return r.results[0]["out_dram"]
```
